# Optimizing a Trainium2 kernel written in Bass

```python
import numpy as np
import jax
import jax.numpy as jnp

def _softmax(x, axis=-1):
    return jax.nn.softmax(x, axis=axis)
def _gelu(x):
    return jax.nn.gelu(x, approximate=True)
def _silu(x):
    return jax.nn.silu(x)
def _sigmoid(x):
    return jax.nn.sigmoid(x)
def _layernorm(x, axis=-1, eps=1e-5):
    m = jnp.mean(x, axis=axis, keepdims=True)
    v = jnp.var(x, axis=axis, keepdims=True)
    return (x - m) / jnp.sqrt(v + eps)
def _scatter_add(tgt, idx, src, axis=0):
    return tgt.at[idx].add(src)
def _segment_sum(src, seg, n):
    return jax.ops.segment_sum(src, seg, n)

kernel_name = 'mk_adj_preln_d1_adj_512_c38185'

def setup_inputs(seed: int = 0):
    np.random.seed(seed)
    _w = jnp.asarray
    def _rec_inputs():
        import jax
        import jax.numpy as jnp
        _gk = jax.random.key(seed)
        x = -0.0005963 + 1.001 * jax.random.normal(jax.random.fold_in(_gk, 1), (6144, 512), jnp.float32)
        _w = (1.0 + jnp.arange(6144, dtype=jnp.float32)) ** -0.5
        _w = _w / _w.mean()
        _pij = jnp.clip(0.000651042 * _w[:, None] * _w[None, :], 0.0, 1.0)
        _a = jax.random.uniform(jax.random.fold_in(_gk, 2), (6144, 6144)) < _pij
        adj = _a.astype(jnp.int32)
        return x, adj
    x, adj = _rec_inputs()
    def _L0_gnn_setup():
        import jax, jax.numpy as jnp
        import numpy as np
        N = 6144
        IN_FEATS = 512
        OUT_FEATS = 64
        NHEADS = 8
        ALPHA = 0.2
        NEG_BIG = -9000000000000000.0
        key = jax.random.key(seed)
        k_x, k_adj, k_w, k_a1, k_a2 = jax.random.split(key, 5)
        x = jax.random.normal(k_x, (N, IN_FEATS), dtype=jnp.float32)
        adj = jax.random.randint(k_adj, (N, N), 0, 2, dtype=jnp.int32)
        gain = 1.414
        bw = gain * np.sqrt(6.0 / (IN_FEATS + OUT_FEATS))
        W = jax.random.uniform(k_w, (NHEADS, IN_FEATS, OUT_FEATS), jnp.float32, -bw, bw)
        ba = gain * np.sqrt(6.0 / (OUT_FEATS + 1))
        a1 = jax.random.uniform(k_a1, (NHEADS, OUT_FEATS), jnp.float32, -ba, ba)
        a2 = jax.random.uniform(k_a2, (NHEADS, OUT_FEATS), jnp.float32, -ba, ba)
        return {'x': x, 'adj': adj, 'W': W, 'a1': a1, 'a2': a2}
    _L0_gnn_all = _L0_gnn_setup()
    _L0_gnn_in = {k: v for k, v in _L0_gnn_all.items() if k in ('W', 'a1', 'a2', )}
    del _L0_gnn_all

    return {
        "x": x,
        "adj": adj,
        "L0_gnn_W": _L0_gnn_in["W"],
        "L0_gnn_a1": _L0_gnn_in["a1"],
        "L0_gnn_a2": _L0_gnn_in["a2"],
    }

def reference(x, adj, L0_gnn_W, L0_gnn_a1, L0_gnn_a2):
    import jax
    import jax.numpy as jnp
    def _L0_gnn_ref(x, adj, W, a1, a2):
        import jax, jax.numpy as jnp
        import numpy as np
        N = 6144
        IN_FEATS = 512
        OUT_FEATS = 64
        NHEADS = 8
        ALPHA = 0.2
        NEG_BIG = -9000000000000000.0
        h = jnp.einsum('ni,hif->hnf', x, W)
        s1 = jnp.einsum('hnf,hf->hn', h, a1)
        s2 = jnp.einsum('hnf,hf->hn', h, a2)
        scores = jax.nn.leaky_relu(s1[:, :, None] + s2[:, None, :], negative_slope=ALPHA)
        scores = jnp.where(adj[None] > 0, scores, NEG_BIG)
        att = jax.nn.softmax(scores, axis=-1)
        out = jnp.einsum('hnm,hmf->hnf', att, h)
        out = jnp.transpose(out, (1, 0, 2)).reshape(N, NHEADS * OUT_FEATS)
        return jax.nn.elu(out)

    h = jnp.maximum(_layernorm(x, axis=-1), 0.0)
    x = x + _L0_gnn_ref(h, adj, L0_gnn_W, L0_gnn_a1, L0_gnn_a2)
    return x


_drawn_inputs = setup_inputs


def setup_inputs(seed=0):
    import zlib

    import numpy as np

    out = dict(_drawn_inputs(seed))
    spreads = {}
    factors = {}
    for name, (base, spread) in spreads.items():
        noise = np.random.default_rng([zlib.crc32(name.encode()), seed]).standard_normal(out[name].shape)
        drawn = base * np.exp(spread * noise) if base else spread * noise
        out[name] = jnp.asarray(drawn.astype(out[name].dtype))
    for name, factor in factors.items():
        out[name] = (out[name] * factor).astype(out[name].dtype)
    return out
```

```python
import concourse.bass as bass
from concourse import mybir
from contextlib import ExitStack

F32 = mybir.dt.float32
BF16 = mybir.dt.bfloat16
I32 = mybir.dt.int32
ALU = mybir.AluOpType
ACT = mybir.ActivationFunctionType
AX = mybir.AxisListType

P = 128
N = 6144
D = 512
H = 8
F = 64
HF = H * F
TILES = N // P
KC = D // P
TABLE = HF + H
EPS = 1e-5
ALPHA = 0.2
NEG_BIG = -9e15


FLAG_SPREAD = 60.0
STEP = 1 << 14
INFO = 2 + 2 * H
GROUP = 1024
GROUPS = N // GROUP


def cuts(shares, inside=(), narrowest=8):
    marks = {0, N} | set(range(0, N, 512)) | set(inside)
    marks |= {narrowest * round(N * (k / shares) ** 2 / narrowest) for k in range(1, shares)}
    marks = sorted(marks)
    kept = [0]
    for m in marks[1:]:
        if m - kept[-1] >= narrowest:
            kept.append(m)
    return list(zip(kept[:-1], kept[1:]))


class Visit:
    def __init__(self, tile, lo, hi, segments, slots, blocks, kind, place, first, last):
        self.tile, self.lo, self.hi, self.slots, self.blocks = tile, lo, hi, slots, blocks
        self.segments = [s for s in segments if lo <= s[0] < hi]
        self.kind, self.place, self.first, self.last = kind, place, first, last


def edge_blocks(tile):
    for start, blocks in ((38, 3), (18, 4), (12, 5), (8, 6), (6, 7), (4, 8), (2, 10)):
        if tile >= start:
            return blocks


def make_visits():
    visits = []
    eighths = [128 * round(N * (k / 8) ** 2 / 128) for k in range(9)]
    fine = cuts(96, eighths)
    for k in range(8):
        visits.append(Visit(0, eighths[k], eighths[k + 1], fine, 40, 4, "A", k, k == 0, k == 7))
    half = cuts(24)
    for k, (lo, hi) in enumerate(((0, 1536), (1536, N))):
        visits.append(Visit(1, lo, hi, half, 24, 7, "B", k, k == 0, k == 1))
    middle = cuts(1, (32, 128, 256))
    for t in range(2, 12):
        visits.append(Visit(t, 0, N, middle, 24, edge_blocks(t), "B", t, True, True))
    wide = [(0, 128), (128, 512), (512, 1024)] + [(g * GROUP, (g + 1) * GROUP) for g in range(1, GROUPS)]
    for t in range(12, TILES):
        visits.append(Visit(t, 0, N, wide, 16, edge_blocks(t), "C", t - 12, True, True))
    return visits


VISITS = make_visits()
V = len(VISITS)
SLOTS = {"A": 40, "B": 24, "C": 16}
COUNT = {"A": 8, "B": 12, "C": 36}
FIRST = {"A": 0, "B": 8, "C": 20}
SEGMENTS = max(len(v.segments) for v in VISITS)
BLOCKS = max(v.blocks for v in VISITS)


def at(count, ref, k):
    return count(ref) if isinstance(k, int) and k == 0 else count(ref) + k * (count(ref + 2) - count(ref))


def broadcast_rows(ap, rows=P):
    return bass.AP(tensor=ap.tensor, offset=ap.offset, ap=[[0, rows]] + list(ap.ap))


def setup(nc, sb, W, a1, a2):
    with ExitStack() as ctx:
        a_rows = ctx.enter_context(nc.sbuf_tensor([P, 2, H, F], F32))
        weighted = ctx.enter_context(nc.sbuf_tensor([P, H, F], F32))
        w_loaded = ctx.enter_context(nc.semaphore())
        a_loaded = ctx.enter_context(nc.semaphore())
        ones_set = ctx.enter_context(nc.semaphore())
        weighted_done = ctx.enter_context(nc.semaphore())
        folded = ctx.enter_context(nc.semaphore())
        block = ctx.enter_context(nc.Block())
        @block.sync
        def _(sp):
            for kc in range(KC):
                sp.dma_start(sb["W"][:, kc, :].rearrange("p (h f) -> p h f", h=H),
                             W[:, kc * P:(kc + 1) * P, :].rearrange("h p f -> p h f")).then_inc(w_loaded, 16)
            sp.dma_start(a_rows[:, 0], broadcast_rows(a1)).then_inc(a_loaded, 16)
            sp.dma_start(a_rows[:, 1], broadcast_rows(a2)).then_inc(a_loaded, 16)

        @block.gpsimd
        def _(pool):
            nc.gpsimd.memset(sb["ones"][:], 1.0).then_inc(ones_set, 1)
            pool.wait_ge(ones_set, 1)
            nc.gpsimd.affine_select(out=sb["ident"][:], in_=sb["ones"][:], compare_op=ALU.is_equal, fill=0.0,
                                    base=0, pattern=[[-1, P]], channel_multiplier=1).then_inc(ones_set, 1)

        @block.vector
        def _(dve):
            dve.wait_ge(w_loaded, 16 * KC)
            dve.wait_ge(a_loaded, 32)
            n = 0
            for kc in range(KC):
                for which in range(2):
                    if n:
                        dve.wait_ge(folded, n)
                    nc.vector.tensor_tensor(weighted[:], sb["W"][:, kc, :].rearrange("p (h f) -> p h f", h=H),
                                            a_rows[:, which], ALU.mult).then_inc(weighted_done, 1)
                    n += 1
                    dve.wait_ge(weighted_done, n)
                    nc.vector.tensor_reduce(sb["Wa"][:, kc, which * H:(which + 1) * H], weighted[:],
                                            AX.X, ALU.add).then_inc(folded, 1)


def scan_constants(nc, sb):
    with ExitStack() as ctx:
        column = ctx.enter_context(nc.sbuf_tensor([2, N], I32))
        shifted = ctx.enter_context(nc.sbuf_tensor([2, N], I32))
        row = ctx.enter_context(nc.sbuf_tensor([2, 1], F32))
        radix_f = ctx.enter_context(nc.sbuf_tensor([2, P], F32))
        digits_f = ctx.enter_context(nc.sbuf_tensor([2, N], F32))
        back = ctx.enter_context(nc.sbuf_tensor([2, N], I32))
        hi = ctx.enter_context(nc.sbuf_tensor([2, N], F32))
        made = ctx.enter_context(nc.semaphore("made"))
        step = ctx.enter_context(nc.semaphore("step"))
        block = ctx.enter_context(nc.Block())

        @block.gpsimd
        def _(pool):
            nc.gpsimd.iota(column[:], [[-1, N]], base=N, channel_multiplier=0).then_inc(made, 1)
            nc.gpsimd.iota(row[:], [[0, 1]], base=0, channel_multiplier=1, allow_small_or_imprecise_dtypes=True).then_inc(made, 1)

        @block.vector
        def _(dve):
            dve.wait_ge(made, 2)
            nc.vector.tensor_scalar(sb["step_diag"][:], sb["ident"][:], float(STEP), None, ALU.mult).then_inc(step, 1)
            nc.vector.tensor_scalar(radix_f[:], sb["ones"][0:2, :], row[:, 0:1], -255.0, ALU.mult, ALU.mult).then_inc(step, 1)
            dve.wait_ge(step, 2)
            nc.vector.tensor_scalar(sb["radix"][:], radix_f[:], 256.0, None, ALU.add).then_inc(step, 1)
            nc.vector.tensor_scalar(shifted[:], column[:], 8, None, ALU.logical_shift_right).then_inc(step, 1)
            dve.wait_ge(step, 4)
            nc.vector.tensor_copy(hi[:], shifted[:]).then_inc(step, 1)
            nc.vector.tensor_copy(digits_f[:], column[:]).then_inc(step, 1)
            dve.wait_ge(step, 6)
            nc.vector.scalar_tensor_tensor(digits_f[:], hi[:], -256.0, digits_f[:], ALU.mult, ALU.add).then_inc(step, 1)
            dve.wait_ge(step, 7)
            nc.vector.tensor_tensor(hi[:], hi[:], digits_f[:], ALU.subtract).then_inc(step, 1)
            nc.vector.tensor_scalar(row[:], row[:], -1.0, 1.0, ALU.mult, ALU.add).then_inc(step, 1)
            dve.wait_ge(step, 9)
            nc.vector.scalar_tensor_tensor(sb["digits"][:], hi[:], row[:, 0:1], digits_f[:], ALU.mult, ALU.add).then_inc(step, 1)


def project_and_scan(nc, sb, x, adj, table):
    HALF = TILES // 2
    PLAN = [("tile", 0), ("tile", 1), ("tile", 2), ("tile", 3), ("loop", 4, 12), ("loop", 12, TILES)]
    of_tile = [[v for v in VISITS if v.tile == t] for t in range(TILES)]
    with ExitStack() as ctx:
        def buf(name, shape, dtype=F32):
            return ctx.enter_context(nc.sbuf_tensor(name, shape, dtype))

        def psum(name, shape):
            return ctx.enter_context(nc.psum_tensor(name, shape, F32))

        def sem(name):
            return ctx.enter_context(nc.semaphore(name))
        x_rows, stats = buf("x_rows", [P, 2, D]), buf("stats", [P, 2, 6])
        both, gap = buf("both", [P, 2, 3]), buf("gap", [P, 2, 2])
        var_eps, std, rstd, shift = (buf(n, [P, 2, 1]) for n in ("var_eps", "std", "rstd", "shift"))
        normed, normedT, h_rows = buf("normed", [P, 2, D]), buf("normedT", [P, 2, KC, P]), buf("h_rows", [P, 2, TABLE])
        adj_rows, adj_bf = buf("adj_rows", [P, 2, N], I32), buf("adj_bf", [P, 2, N], BF16)
        cands = buf("cands", [P, SEGMENTS * 8])
        found = buf("found", [P, max(SLOTS.values())])
        psK, psT = psum("psK", [P, 2, GROUP]), psum("psT", [P, KC, P])
        psH, psS = psum("psH", [P, 2, HF]), psum("psS", [P, 512])
        x_loaded, stored, adj_loaded = ([sem(f"{n}{u}") for u in range(2)] for n in ("x_loaded", "stored", "adj_loaded"))
        stats_done, moments_done, var_done, std_done = sem("stats_done"), sem("moments_done"), sem("var_done"), sem("std_done")
        rstd_done, shift_done, norm_done = sem("rstd_done"), sem("shift_done"), sem("norm_done")
        transposed, normedT_done, projected = sem("transposed"), sem("normedT_done"), sem("projected")
        h_copied, s_copied, added = sem("h_copied"), sem("s_copied"), sem("added")
        adj_converted, keys_ready, keys_read = sem("adj_converted"), sem("keys_ready"), sem("keys_read")
        segments_done, cands_cut, slots_done, scan_turn = sem("segments_done"), sem("cands_cut"), sem("slots_done"), sem("scan_turn")
        sum_cleared, key_turn = sem("sum_cleared"), sem("key_turn")
        block = ctx.enter_context(nc.Block())
        xt = x.rearrange("(t p) d -> t p d", p=P)
        adjt = adj.rearrange("(t p) n -> t p n", p=P)
        tt = table[0:N].rearrange("(t p) d -> t p d", p=P)

        def tile_at(ap, t):
            return ap[t] if isinstance(t, int) else ap[bass.ds(t, 1)][0]

        def walk(eng, body):
            for kind, *span in PLAN:
                if kind == "tile":
                    body(span[0], 0)
                else:
                    with eng.Fori(0, (span[1] - span[0]) // 2) as k:
                        for u in range(2):
                            body(span[0] + u, k)

        def pairs(t):
            return 16 * (t // 2 + 1)

        @block.sync
        def _(sp):
            for u in range(2):
                sp.dma_start(x_rows[:, u], xt[u]).then_inc(x_loaded[u], 16)
                sp.dma_start(adj_rows[:, u], adjt[u]).then_inc(adj_loaded[u], 16)

            def body(ref, k):
                t, u = ref + 2 * k, ref % 2
                if ref >= 2:
                    sp.wait_ge(norm_done, t - 1)
                    sp.dma_start(x_rows[:, u], tile_at(xt, t)).then_inc(x_loaded[u], 16)
                    sp.wait_ge(adj_converted, GROUPS * (t - 1))
                    sp.dma_start(adj_rows[:, u], tile_at(adjt, t)).then_inc(adj_loaded[u], 16)
                if ref >= 2:
                    sp.wait_ge(h_copied, t - 1)
                    sp.wait_ge(s_copied, t - 1)
                    sp.dma_start(tile_at(tt, t - 2), h_rows[:, u]).then_inc(stored[u], 16)
            walk(sp, body)
            for t in (TILES - 2, TILES - 1):
                sp.wait_ge(h_copied, t + 1)
                sp.wait_ge(s_copied, t + 1)
                sp.dma_start(tt[t], h_rows[:, t % 2]).then_inc(stored[t % 2], 16)
            for u in range(2):
                sp.wait_ge(stored[u], 16 * HALF)

        def seg_count(t):
            return sum(len(v.segments) for v in VISITS if v.tile < t)

        def cut_count(t):
            return sum(2 * (v.slots // 8) - 1 for v in VISITS if v.tile < t)

        def visit_count(t):
            return sum(1 for v in VISITS if v.tile < t)

        @block.vector
        def _(dve):
            nc.vector.memset(sb["node_sum"][:], 0.0).then_inc(sum_cleared, 1)

            def body(ref, k):
                t, u = ref + 2 * k, ref % 2
                dve.wait_ge(x_loaded[u], at(pairs, ref, k))
                nc.vector.bn_stats(stats[:, u], x_rows[:, u]).then_inc(stats_done, 1)
                dve.wait_ge(stats_done, t + 1)
                nc.vector.tensor_tensor(both[:, u], stats[:, u, 0:3], stats[:, u, 3:6], ALU.add).then_inc(moments_done, 1)
                nc.vector.tensor_tensor(gap[:, u, 0:1], stats[:, u, 4:5], stats[:, u, 1:2], ALU.subtract).then_inc(moments_done, 1)
                dve.wait_ge(moments_done, 4 * t + 2)
                nc.vector.tensor_scalar(both[:, u, 0:1], both[:, u, 2:3], 1.0 / D, EPS, ALU.mult, ALU.add).then_inc(moments_done, 1)
                nc.vector.scalar_tensor_tensor(gap[:, u, 1:2], gap[:, u, 0:1], 0.25, gap[:, u, 0:1],
                                               ALU.mult, ALU.mult).then_inc(moments_done, 1)
                dve.wait_ge(moments_done, 4 * t + 4)
                nc.vector.tensor_tensor(var_eps[:, u], both[:, u, 0:1], gap[:, u, 1:2], ALU.add).then_inc(var_done, 1)
                n_seg = 0
                per_visit = [0] * len(of_tile[ref])
                visits = of_tile[ref]
                cut = 0

                def rank(which, v):
                    nonlocal cut
                    nc_ = len(v.segments) * 8
                    number = visit_count(ref) + which
                    dve.wait_ge(segments_done, at(seg_count, ref, k) + n_seg)
                    dve.sem_inc(scan_turn, 1)
                    eighth = cands[:, 0:nc_].rearrange("p (s e) -> p s e", e=8)[:, :, 7]
                    cell = sb["fullest"][:, number:number + 1] if isinstance(k, int) else \
                        sb["fullest"][:, bass.ds(number + 2 * k, 1)]
                    nc.vector.tensor_reduce(cell, eighth, AX.X, ALU.max)
                    for r in range(v.slots // 8):
                        nc.vector.max(found[:, 8 * r:8 * r + 8], cands[:, 0:nc_]).then_inc(cands_cut, 1)
                        cut += 1
                        if r < v.slots // 8 - 1:
                            dve.wait_ge(cands_cut, at(cut_count, ref, k) + cut)
                            dve.sem_inc(scan_turn, 1)
                            nc.vector.match_replace(cands[:, 0:nc_], found[:, 8 * r:8 * r + 8], cands[:, 0:nc_], -1.0).then_inc(cands_cut, 1)
                            cut += 1
                            dve.wait_ge(cands_cut, at(cut_count, ref, k) + cut)
                            dve.sem_inc(scan_turn, 1)
                    dve.wait_ge(cands_cut, at(cut_count, ref, k) + cut)
                    info = sb["info" + v.kind]
                    if isinstance(k, int):
                        dst = info[:, v.place, 0:v.slots]
                    else:
                        dst = info[:, bass.ds(v.place + 2 * k, 1), 0:v.slots].rearrange("p a b -> p (a b)")
                    nc.vector.tensor_scalar(dst, found[:, 0:v.slots], -float(STEP), 0.0, ALU.add, ALU.max).then_inc(slots_done, 1)

                for g in range(GROUPS):
                    dve.wait_ge(keys_ready, GROUPS * t + g + 1)
                    dve.sem_inc(scan_turn, 1)
                    last = None
                    for which, v in enumerate(visits):
                        segs = [s for s in v.segments if s[0] // GROUP == g]
                        for lo, hi in segs:
                            j = per_visit[which]
                            last = nc.vector.max(cands[:, 8 * j:8 * j + 8], psK[:, g % 2, lo - g * GROUP:hi - g * GROUP])
                            per_visit[which] += 1
                            n_seg += 1
                            last.then_inc(segments_done, 1)
                        if segs and per_visit[which] == len(v.segments):
                            rank(which, v)
                    dve.wait_ge(segments_done, at(seg_count, ref, k) + n_seg)
                    dve.sem_inc(keys_read, 1)
                    if g == 1:
                        dve.wait_ge(std_done, t + 1)
                        if ref >= 2:
                            dve.wait_ge(norm_done, t - 1)
                        nc.vector.reciprocal(rstd[:, u], std[:, u]).then_inc(rstd_done, 1)
                        dve.wait_ge(rstd_done, t + 1)
                        nc.vector.scalar_tensor_tensor(shift[:, u], both[:, u, 1:2], -0.5, rstd[:, u],
                                                       ALU.mult, ALU.mult).then_inc(shift_done, 1)
                if ref >= 1:
                    scores(ref - 1, k)

            def scores(ref, k):
                t, u = ref + 2 * k, ref % 2
                dve.wait_ge(projected, t + 1)
                if ref >= 2:
                    dve.wait_ge(stored[u], at(pairs, ref - 2, k))
                nc.vector.tensor_copy(h_rows[:, u, HF:TABLE], psS[:, H:2 * H])
                if isinstance(k, int):
                    to1, to2 = sb["s1"][:, t], sb["s2"][:, t]
                else:
                    to1, to2 = (sb[n][:, bass.ds(t, 1)].rearrange("p a b -> p (a b)") for n in ("s1", "s2"))
                nc.vector.tensor_copy(to1, psS[:, 0:H])
                nc.vector.tensor_copy(to2, psS[:, H:2 * H]).then_inc(s_copied, 1)

            walk(dve, body)
            scores(TILES - 1, 0)

        @block.scalar
        def _(act):
            def convert(ref, k, g):
                t, u = ref + 2 * k, ref % 2
                if g == 0:
                    act.wait_ge(adj_loaded[u], at(pairs, ref, k))
                if ref >= 2:
                    act.wait_ge(keys_ready, GROUPS * (t - 2) + g + 1)
                nc.scalar.activation(adj_bf[:, u, g * GROUP:(g + 1) * GROUP], adj_rows[:, u, g * GROUP:(g + 1) * GROUP],
                                     ACT.Copy).then_inc(adj_converted, 1)

            def h_out(ref, k):
                t, u = ref + 2 * k, ref % 2
                act.wait_ge(projected, t + 1)
                if ref >= 2:
                    act.wait_ge(stored[u], at(pairs, ref - 2, k))
                    act.wait_ge(added, t - 1)
                nc.scalar.activation(h_rows[:, u, 0:HF], psH[:, u], ACT.Copy).then_inc(h_copied, 1)

            def body(ref, k):
                t, u = ref + 2 * k, ref % 2
                convert(ref, k, 0)
                convert(ref, k, 1)
                act.wait_ge(var_done, t + 1)
                nc.scalar.activation(std[:, u], var_eps[:, u], ACT.Sqrt).then_inc(std_done, 1)
                convert(ref, k, 2)
                convert(ref, k, 3)
                act.wait_ge(shift_done, t + 1)
                if ref >= 2:
                    act.wait_ge(transposed, t - 1)
                nc.scalar.activation(normed[:, u], x_rows[:, u], ACT.Relu, bias=shift[:, u],
                                     scale=rstd[:, u]).then_inc(norm_done, 1)
                convert(ref, k, 4)
                convert(ref, k, 5)
                if ref >= 1:
                    h_out(ref - 1, k)
                act.wait_ge(transposed, t + 1)
                if ref >= 2:
                    act.wait_ge(projected, t - 1)
                nc.scalar.activation(normedT[:, u], psT[:], ACT.Copy).then_inc(normedT_done, 1)
            walk(act, body)
            h_out(TILES - 1, 0)

        @block.tensor
        def _(pe):
            def keys(ref, k, g):
                t, u = ref + 2 * k, ref % 2
                pe.wait_ge(adj_converted, GROUPS * t + g + 1)
                if not (isinstance(k, int) and ref == 0 and g < 2):
                    pe.wait_ge(keys_read, GROUPS * t + g - 1)
                pe.sem_inc(key_turn, 1)
                for b in range(GROUP // 512):
                    c = g * GROUP + b * 512
                    nc.tensor.matmul(psK[:, g % 2, b * 512:(b + 1) * 512], sb["step_diag"][:], adj_bf[:, u, c:c + 512],
                                     start=True, stop=False)
                    mm = nc.tensor.matmul(psK[:, g % 2, b * 512:(b + 1) * 512], sb["radix"][:], sb["digits"][:, c:c + 512],
                                          start=False, stop=True)
                mm.then_inc(keys_ready, 1)

            def project_slice(ref, k, kc):
                t, u = ref + 2 * k, ref % 2
                if kc == 0:
                    pe.wait_ge(normedT_done, t + 1)
                    if ref >= 1:
                        pe.wait_ge(s_copied, t)
                    if ref >= 2:
                        pe.wait_ge(h_copied, t - 1)
                nc.tensor.matmul(psH[:, u], normedT[:, u, kc], sb["W"][:, kc], start=(kc == 0), stop=(kc == KC - 1))
                mm = nc.tensor.matmul(psS[:, 0:2 * H], normedT[:, u, kc], sb["Wa"][:, kc],
                                      start=(kc == 0), stop=(kc == KC - 1))
                if kc == KC - 1:
                    mm.then_inc(projected, 1)

            def body(ref, k):
                t, u = ref + 2 * k, ref % 2
                for g in range(GROUPS):
                    keys(ref, k, g)
                    if ref >= 1 and g < KC:
                        project_slice(ref - 1, k, g)
                    if g == 4:
                        pe.wait_ge(norm_done, t + 1)
                        if ref >= 1:
                            pe.wait_ge(normedT_done, t)
                        for kc in range(KC):
                            mm = nc.tensor.transpose(psT[:, kc], normed[:, u, kc * P:(kc + 1) * P], sb["ident"][:])
                        mm.then_inc(transposed, 1)
            walk(pe, body)
            for kc in range(KC):
                project_slice(TILES - 1, 0, kc)

        @block.gpsimd
        def _(pool):
            pool.wait_ge(sum_cleared, 1)

            def body(ref, k):
                t, u = ref + 2 * k, ref % 2
                pool.wait_ge(h_copied, t + 1)
                if ref >= 1:
                    pool.wait_ge(added, t)
                nc.gpsimd.tensor_tensor(sb["node_sum"][:], sb["node_sum"][:], h_rows[:, u, 0:HF], ALU.add).then_inc(added, 1)
            walk(pool, body)


def plan(nc, sb, table):
    with ExitStack() as ctx:
        def buf(name, shape, dtype=F32):
            return ctx.enter_context(nc.sbuf_tensor(name, shape, dtype))

        def sem(name):
            return ctx.enter_context(nc.semaphore(name))
        used = {kind: buf("used" + kind, [P, COUNT[kind], SLOTS[kind]]) for kind in "ABC"}
        degree, total, half = buf("degree", [P, V]), buf("total", [P, 2]), buf("half", [P, V])
        earlier, row_no = buf("earlier", [P, P]), buf("row_no", [P, 1])
        most, hi_lo, ext = buf("most", [P, 2 * H]), buf("hi_lo", [H, 2]), buf("ext", [H, 2 * H])
        bound8, spread = buf("bound8", [P, 2 * H]), buf("spread", [P, H])
        raw, bound = buf("raw", [P, TILES, H]), buf("bound", [P, TILES, H])
        flags, worst = buf("flags", [P, 4 * V + H]), buf("worst", [P, 1])
        mean_row, flag_f = buf("mean_row", [1, TABLE]), buf("flag_f", [1, 1])
        psA = ctx.enter_context(nc.psum_tensor("psA", [P, 512], F32))
        psB = ctx.enter_context(nc.psum_tensor("psB", [P, 512], F32))
        psC = ctx.enter_context(nc.psum_tensor("psC2", [P, 512], F32))
        psD = ctx.enter_context(nc.psum_tensor("psD2", [P, 512], F32))
        made, step, summed, stored = sem("made"), sem("step"), sem("summed"), sem("mean_stored")
        degrees_ready, extremes_ready = sem("degrees_ready"), sem("extremes_ready")
        worst_ready, mean_ready = sem("worst_ready"), sem("mean_ready")
        block = ctx.enter_context(nc.Block())

        @block.gpsimd
        def _(pool):
            nc.gpsimd.affine_select(out=earlier[:], in_=sb["ones"][:], compare_op=ALU.is_gt, fill=0.0,
                                    base=0, pattern=[[1, P]], channel_multiplier=-1).then_inc(made, 1)
            nc.gpsimd.iota(row_no[:], [[0, 1]], base=1, channel_multiplier=1, allow_small_or_imprecise_dtypes=True).then_inc(made, 1)

        @block.vector
        def _(dve):
            n = [0]

            def did(ins):
                n[0] += 1
                ins.then_inc(step, 1)

            def settle():
                dve.wait_ge(step, n[0])
            for kind in "ABC":
                did(nc.vector.tensor_scalar(used[kind][:], sb["info" + kind][:, :, 0:SLOTS[kind]], 0.0, None, ALU.is_gt))
            did(nc.vector.tensor_reduce(most[:, 0:H], sb["s2"][:].rearrange("p t h -> p h t"), AX.X, ALU.max))
            did(nc.vector.tensor_reduce(most[:, H:2 * H], sb["s2"][:].rearrange("p t h -> p h t"), AX.X, ALU.min))
            settle()
            for kind in "ABC":
                f, c = FIRST[kind], COUNT[kind]
                did(nc.vector.tensor_reduce(degree[:, f:f + c], used[kind][:], AX.X, ALU.add))
            settle()
            did(nc.vector.tensor_reduce(total[:, 0:1], degree[:, 0:8], AX.X, ALU.add))
            did(nc.vector.tensor_reduce(total[:, 1:2], degree[:, 8:10], AX.X, ALU.add))
            settle()
            did(nc.vector.scalar_tensor_tensor(degree[:, 0:1], total[:, 0:1], 0.0, degree[:, 0:1], ALU.is_equal, ALU.add))
            did(nc.vector.scalar_tensor_tensor(degree[:, 8:9], total[:, 1:2], 0.0, degree[:, 8:9], ALU.is_equal, ALU.add))
            did(nc.vector.scalar_tensor_tensor(degree[:, 10:V], degree[:, 10:V], 0.0, degree[:, 10:V], ALU.is_equal, ALU.add))
            settle()
            dve.sem_inc(degrees_ready, 1)
            dve.wait_ge(summed, 1)
            did(nc.vector.tensor_reduce(hi_lo[:, 0:1], psC[0:H, 0:P], AX.X, ALU.max))
            did(nc.vector.tensor_reduce(hi_lo[:, 1:2], psC[0:H, P:2 * P], AX.X, ALU.min))
            settle()
            did(nc.vector.tensor_scalar(ext[:, 0:H], sb["ident"][0:H, 0:H], hi_lo[:, 0:1], None, ALU.mult))
            did(nc.vector.tensor_scalar(ext[:, H:2 * H], sb["ident"][0:H, 0:H], hi_lo[:, 1:2], None, ALU.mult))
            settle()
            dve.sem_inc(extremes_ready, 1)
            dve.wait_ge(summed, 2)
            did(nc.vector.tensor_scalar(half[:], degree[:], 0.5, None, ALU.mult))
            settle()
            did(nc.vector.tensor_tensor(sb["half_sq"][:], half[:], half[:], ALU.mult))
            did(nc.vector.scalar_tensor_tensor(sb["neg_centre"][:], psA[:, 0:V], 1.0, half[:], ALU.mult, ALU.add))
            settle()
            did(nc.vector.tensor_scalar(sb["neg_centre"][:], sb["neg_centre"][:], -1.0, 0.5, ALU.mult, ALU.add))
            dve.wait_ge(summed, 3)
            did(nc.vector.tensor_copy(bound8[:], psD[:, 0:2 * H]))
            settle()
            did(nc.vector.tensor_tensor(raw[:], sb["s1"][:], bound8[:, 0:H].unsqueeze(1).to_broadcast([P, TILES, H]), ALU.add))
            did(nc.vector.tensor_tensor(spread[:], bound8[:, 0:H], bound8[:, H:2 * H], ALU.subtract))
            settle()
            did(nc.vector.scalar_tensor_tensor(bound[:].rearrange("p t h -> p (t h)"), raw[:].rearrange("p t h -> p (t h)"), ALPHA,
                                               raw[:].rearrange("p t h -> p (t h)"), ALU.mult, ALU.max))
            dve.wait_ge(made, 2)
            settle()
            for kind in "ABC":
                f, c, s = FIRST[kind], COUNT[kind], SLOTS[kind]
                info = sb["info" + kind]
                did(nc.vector.tensor_copy(info[:, :, s:s + 1], psA[:, f:f + c].unsqueeze(2)))
                did(nc.vector.tensor_copy(info[:, :, s + 1:s + 2], row_no[:].unsqueeze(2).to_broadcast([P, c, 1])))
                shares = {"A": [(0, 8, 0, 1)], "B": [(0, 2, 1, 1), (2, 12, 2, 10)], "C": [(0, 36, 12, 36)]}[kind]
                for p0, p1, t0, nt in shares:
                    for src, o in ((sb["s1"], 2), (bound, 2 + H)):
                        part = src[:, t0:t0 + nt]
                        if nt != p1 - p0:
                            part = part.to_broadcast([P, p1 - p0, H])
                        did(nc.vector.tensor_copy(info[:, p0:p1, s + o:s + o + H], part))
                did(nc.vector.tensor_scalar(flags[:, f:f + c], info[:, :, s - 1], 0.0, None, ALU.is_gt))
                did(nc.vector.tensor_scalar(flags[:, V + f:V + f + c], info[:, :, 0], STEP / 2.0, None, ALU.is_gt))
            did(nc.vector.tensor_scalar(flags[:, 2 * V:3 * V], sb["fullest"][:], float(STEP), None, ALU.is_ge))
            v0 = 0
            while v0 < V:
                v1 = v0
                while v1 < V and VISITS[v1].blocks == VISITS[v0].blocks:
                    v1 += 1
                did(nc.vector.tensor_scalar(flags[:, 3 * V + v0:3 * V + v1], psB[:, v0:v1], float(P * VISITS[v0].blocks), None, ALU.is_gt))
                v0 = v1
            did(nc.vector.tensor_scalar(flags[:, 4 * V:], spread[:], FLAG_SPREAD, None, ALU.is_gt))
            settle()
            did(nc.vector.tensor_reduce(worst[:], flags[:], AX.X, ALU.max))
            settle()
            dve.sem_inc(worst_ready, 1)
            dve.wait_ge(summed, 4)
            did(nc.vector.tensor_scalar(mean_row[:, 0:HF], psC[0:1, 0:HF], 1.0 / N, None, ALU.mult))
            did(nc.vector.tensor_copy(mean_row[:, HF:TABLE], bound8[0:1, 0:H]))
            settle()
            dve.sem_inc(mean_ready, 1)
            dve.wait_ge(summed, 5)
            did(nc.vector.tensor_scalar(flag_f[:], psA[0:1, 0:1], 0.0, None, ALU.is_gt))
            settle()
            nc.vector.tensor_copy(sb["flag"][:], flag_f[:]).then_inc(step, 1)

        @block.tensor
        def _(pe):
            pe.wait_ge(degrees_ready, 1)
            nc.tensor.transpose(psC[0:H, 0:P], most[:, 0:H], sb["ident"][:])
            nc.tensor.transpose(psC[0:H, P:2 * P], most[:, H:2 * H], sb["ident"][:]).then_inc(summed, 1)
            pe.wait_ge(made, 1)
            nc.tensor.matmul(psA[:, 0:V], earlier[:], degree[:], start=True, stop=True)
            nc.tensor.matmul(psB[:, 0:V], sb["ones"][:], degree[:], start=True, stop=True).then_inc(summed, 1)
            pe.wait_ge(extremes_ready, 1)
            nc.tensor.matmul(psD[:, 0:2 * H], sb["ones"][0:H, :], ext[:], start=True, stop=True).then_inc(summed, 1)
            nc.tensor.matmul(psC[:, 0:HF], sb["ones"][:], sb["node_sum"][:], start=True, stop=True).then_inc(summed, 1)
            pe.wait_ge(worst_ready, 1)
            nc.tensor.matmul(psA[0:1, 0:1], worst[:], sb["ones"][:, 0:1], start=True, stop=True).then_inc(summed, 1)

        @block.sync
        def _(sp):
            sp.wait_ge(mean_ready, 1)
            sp.dma_start(table[N:N + 1], mean_row[:]).then_inc(stored, 16)
            sp.wait_ge(stored, 16)


def attend_edges(nc, sb, x, table, out):
    with ExitStack() as ctx:
        def buf(name, shape, dtype=F32):
            return ctx.enter_context(nc.sbuf_tensor(name, shape, dtype))

        def psum(name, shape):
            return ctx.enter_context(nc.psum_tensor(name, shape, F32))

        def sem(name):
            return ctx.enter_context(nc.semaphore(name))
        edge_no = buf("edge_no", [P, BLOCKS * P])
        list_no = buf("list_no", [P, BLOCKS])
        distance, owner = buf("distance", [P, 2, BLOCKS * P]), buf("owner", [P, 2, BLOCKS * P])
        facts = buf("facts", [P, 2, 512])
        slot = buf("slot", [P, BLOCKS])
        chosen = buf("chosen", [P, BLOCKS * 24])
        key, column = buf("key", [P, BLOCKS]), buf("column", [P, 2, BLOCKS], mybir.dt.uint32)
        nodes = buf("nodes", [P, 2, BLOCKS, TABLE])
        to_row = buf("to_row", [P, 2, BLOCKS, P])
        score, weight = buf("score", [P, 3, BLOCKS, H]), buf("weight", [P, 2, BLOCKS, H])
        recip, agg = buf("recip", [P, H]), buf("agg", [P, HF])
        x_part, grown, kept, result = (buf(n, [P, 2, HF]) for n in ("x_part", "grown", "kept", "result"))
        psC, psO, psD = psum("psC", [P, 2, 512]), psum("psO", [P, 2, HF]), psum("psD", [P, 2, 512])
        gathered, x_loaded, stored = ([sem(f"{n}{u}") for u in range(2)] for n in ("gathered", "xe_loaded", "out_stored"))
        made = sem("counted")
        squared, owners, looked_up, facts_done = sem("squared"), sem("owners"), sem("looked_up"), sem("facts_done")
        front_step, columns, back_step, shifted = sem("front_step"), sem("columns"), sem("back_step"), sem("shifted")
        to_row_done, weights, weighted, summed = sem("to_row_done"), sem("weights"), sem("weighted"), sem("rows_summed")
        end_step, agg_done, grown_done, finished = sem("end_step"), sem("agg_done"), sem("grown_done"), sem("finished")
        act_turn, pool_turn, less_one = sem("act_turn"), sem("pool_turn"), sem("less_one")
        block = ctx.enter_context(nc.Block())
        xt = x.rearrange("(t p) d -> t p d", p=P)
        ot = out.rearrange("(t p) d -> t p d", p=P)

        def tile_at(ap, t):
            return ap[t] if isinstance(t, int) else ap[bass.ds(t, 1)][0]

        def same(a, b):
            return VISITS[a].blocks == VISITS[b].blocks and VISITS[a].kind == VISITS[b].kind

        def walk(eng, body):
            v = 0
            while v <= V:
                end = v
                if v % 2 == 0 and v >= 12:
                    while end + 3 < V and same(v - 1, end) and same(v - 1, end + 3) and same(v - 1, v + 2):
                        end += 2
                if end > v + 2:
                    with eng.Fori(0, (end - v) // 2) as k:
                        for u in range(2):
                            body(v + u, k)
                    v = end
                else:
                    body(v, 0)
                    v += 1

        def one(v):
            return v + 1

        def tiles_ended(v):
            return sum(1 for w in VISITS[:v + 1] if w.last) if v < V else tiles_ended(V - 1) + v - V + 1

        def landed(v):
            return 16 * sum(w.blocks for w in VISITS[v % 2:v + 1:2])

        def looked(array, u, w):
            width = w.slots + INFO
            return array[:, u, 0:w.blocks * width].rearrange("p (q c) -> p q c", c=width)

        def info_of(ref, k):
            v = VISITS[ref]
            info = sb["info" + v.kind]
            if isinstance(k, int):
                return info[:, v.place]
            return info[:, bass.ds(v.place + 2 * k, 1)].rearrange("p a b -> p (a b)")

        def column_of(array, ref, k):
            return array[:, ref:ref + 1] if isinstance(k, int) else array[:, bass.ds(ref + 2 * k, 1)]

        @block.gpsimd
        def _(pool):
            nc.gpsimd.iota(edge_no[:], [[1, BLOCKS * P]], base=0, channel_multiplier=0, allow_small_or_imprecise_dtypes=True).then_inc(made, 1)
            nc.gpsimd.iota(list_no[:], [[P, BLOCKS]], base=0, channel_multiplier=1, allow_small_or_imprecise_dtypes=True).then_inc(made, 1)

            def gather(ref, k):
                v, u = ref + 2 * k, ref % 2
                pool.wait_ge(columns, v + 1)
                if ref >= 2:
                    pool.wait_ge(summed, v - 1)
                pool.sem_inc(pool_turn, 1)
                for q in range(VISITS[ref].blocks):
                    nc.gpsimd.indirect_dma_start(out=nodes[:, u, q], out_offset=None, in_=table,
                                                 in_offset=bass.IndirectOffsetOnAxis(ap=column[:, u, q:q + 1], axis=0)
                                                 ).then_inc(gathered[u], 16)

            gather(0, 0)

            def body(ref, k):
                if ref + 1 < V:
                    gather(ref + 1, k)
            walk(pool, body)

        @block.sync
        def _(sp):
            def body(ref, k):
                if ref < V and VISITS[ref].last:
                    n = tiles_ended(ref)
                    u = (n - 1) % 2
                    t = n - 1 + 2 * k
                    if n > 2:
                        sp.wait_ge(finished, t - 1)
                    sp.dma_start(x_part[:, u], tile_at(xt, t)).then_inc(x_loaded[u], 16)
                if ref >= 2 and VISITS[ref - 2].last:
                    n = tiles_ended(ref - 2)
                    u = (n - 1) % 2
                    t = n - 1 + 2 * k
                    sp.wait_ge(finished, t + 1)
                    sp.dma_start(tile_at(ot, t), result[:, u]).then_inc(stored[u], 16)
            walk(sp, body)
            body(V + 1, 0)
            for u in range(2):
                sp.wait_ge(stored[u], 16 * (TILES // 2))

        @block.scalar
        def _(act):
            act.wait_ge(made, 1)

            def square(ref, k):
                v, u, q = ref + 2 * k, ref % 2, VISITS[ref].blocks
                if ref >= 2:
                    act.wait_ge(owners, v - 1)
                act.sem_inc(act_turn, 1)
                nc.scalar.activation(distance[:, u, 0:q * P], edge_no[:, 0:q * P], ACT.Square,
                                     bias=column_of(sb["neg_centre"], ref, k)).then_inc(squared, 1)

            def body(ref, k):
                v, u = ref + 2 * k, ref % 2
                if ref + 2 < V:
                    square(ref + 2, k)
                if ref + 1 < V:
                    w = VISITS[ref + 1]
                    act.wait_ge(looked_up, v + 2)
                    if ref >= 1:
                        act.wait_ge(shifted, v)
                        act.wait_ge(to_row_done, v)
                    nc.scalar.activation(looked(facts, 1 - u, w), looked(psC, 1 - u, w), ACT.Copy).then_inc(facts_done, 1)
                if ref < V:
                    q = VISITS[ref].blocks
                    act.wait_ge(shifted, v + 1)
                    if ref >= 2:
                        act.wait_ge(summed, v - 1)
                    nc.scalar.activation(weight[:, u, 0:q], score[:, 2, 0:q], ACT.Exp).then_inc(weights, 1)
                if ref >= 1 and VISITS[ref - 1].last:
                    n = tiles_ended(ref - 1)
                    t = n - 1 + 2 * k
                    act.wait_ge(agg_done, t + 1)
                    nc.scalar.activation(grown[:, (n - 1) % 2], agg[:], ACT.Exp).then_inc(grown_done, 1)
            square(0, 0)
            square(1, 0)
            act.wait_ge(looked_up, 1)
            w = VISITS[0]
            nc.scalar.activation(looked(facts, 0, w), looked(psC, 0, w), ACT.Copy).then_inc(facts_done, 1)
            walk(act, body)

        @block.vector
        def _(dve):
            dve.wait_ge(made, 2)

            def own(ref, k):
                v, u, q = ref + 2 * k, ref % 2, VISITS[ref].blocks
                dve.wait_ge(squared, v + 1)
                if ref >= 2:
                    dve.wait_ge(looked_up, v - 1)
                nc.vector.tensor_scalar(owner[:, u, 0:q * P], distance[:, u, 0:q * P], column_of(sb["half_sq"], ref, k),
                                        None, ALU.is_lt).then_inc(owners, 1)

            def front(ref, k):
                v, u = ref + 2 * k, ref % 2
                w = VISITS[ref]
                q, s = w.blocks, w.slots
                rows = looked(facts, u, w)
                dve.wait_ge(facts_done, v + 1)
                nc.vector.tensor_tensor(slot[:, 0:q], list_no[:, 0:q], rows[:, :, s], ALU.subtract).then_inc(front_step, 1)
                dve.wait_ge(front_step, 4 * v + 1)
                pick = chosen[:, 0:q * s].rearrange("p (q s) -> p q s", s=s)
                nc.vector.tensor_tensor(pick, edge_no[:, 0:s].unsqueeze(1).to_broadcast([P, q, s]),
                                        slot[:, 0:q].unsqueeze(2).to_broadcast([P, q, s]), ALU.is_equal).then_inc(front_step, 1)
                dve.wait_ge(front_step, 4 * v + 2)
                nc.vector.tensor_tensor(pick, pick, rows[:, :, 0:s], ALU.mult).then_inc(front_step, 1)
                dve.wait_ge(front_step, 4 * v + 3)
                nc.vector.tensor_reduce(key[:, 0:q], pick, AX.X, ALU.add).then_inc(front_step, 1)
                dve.wait_ge(front_step, 4 * v + 4)
                if ref >= 2:
                    dve.wait_ge(gathered[u], at(landed, ref - 2, k))
                nc.vector.tensor_scalar(column[:, u, 0:q], key[:, 0:q], -1.0, float(N), ALU.mult, ALU.add).then_inc(columns, 1)

            def back(ref, k):
                v, u, q, s = ref + 2 * k, ref % 2, VISITS[ref].blocks, VISITS[ref].slots
                rows = looked(facts, u, VISITS[ref])
                dve.wait_ge(gathered[u], at(landed, ref, k))
                nc.vector.tensor_tensor(score[:, 0, 0:q], nodes[:, u, 0:q, HF:TABLE], rows[:, :, s + 2:s + 2 + H],
                                        ALU.add).then_inc(back_step, 1)
                dve.wait_ge(back_step, 2 * v + 1)
                nc.vector.scalar_tensor_tensor(score[:, 1, 0:q], score[:, 0, 0:q], ALPHA, score[:, 0, 0:q],
                                               ALU.mult, ALU.max).then_inc(back_step, 1)
                dve.wait_ge(back_step, 2 * v + 2)
                if ref >= 1:
                    dve.wait_ge(weights, v)
                nc.vector.tensor_tensor(score[:, 2, 0:q], score[:, 1, 0:q], rows[:, :, s + 2 + H:s + INFO],
                                        ALU.subtract).then_inc(shifted, 1)
                if ref >= 2:
                    dve.wait_ge(summed, v - 1)
                nc.vector.tensor_tensor(to_row[:, u, 0:q], edge_no[:, 1:P + 1].unsqueeze(1).to_broadcast([P, q, P]),
                                        rows[:, :, s + 1:s + 2].to_broadcast([P, q, P]), ALU.is_equal).then_inc(to_row_done, 1)
                dve.wait_ge(weights, v + 1)
                by_head = nodes[:, u, 0:q, 0:HF].rearrange("p q (h f) -> p q h f", h=H)
                nc.vector.tensor_tensor(by_head, by_head, weight[:, u, 0:q].unsqueeze(3).to_broadcast([P, q, H, F]),
                                        ALU.mult).then_inc(weighted, 1)

            def end(ref, k):
                n = tiles_ended(ref)
                t, w, u = n - 1 + 2 * k, (n - 1) % 2, (n - 1) % 2
                v = ref + 2 * k
                dve.wait_ge(summed, v + 1)
                nc.vector.reciprocal(recip[:], psD[:, u, 0:H]).then_inc(end_step, 1)
                dve.wait_ge(end_step, 2 * t + 1)
                if n > 1:
                    dve.wait_ge(grown_done, t)
                nc.vector.tensor_tensor(agg[:].rearrange("p (h f) -> p h f", h=H), psO[:, u].rearrange("p (h f) -> p h f", h=H),
                                        recip[:].unsqueeze(2).to_broadcast([P, H, F]), ALU.mult).then_inc(agg_done, 1)
                dve.wait_ge(agg_done, t + 1)
                dve.wait_ge(x_loaded[u], 16 * (((n - 1) // 2) + 1 + k))
                nc.vector.scalar_tensor_tensor(kept[:, u], agg[:], 0.0, x_part[:, u], ALU.max, ALU.add).then_inc(end_step, 1)
                dve.wait_ge(grown_done, t + 1)
                nc.vector.tensor_scalar(grown[:, u], grown[:, u], 1.0, -1.0, ALU.min, ALU.add).then_inc(less_one, 1)
                dve.wait_ge(less_one, t + 1)
                dve.wait_ge(end_step, 2 * t + 2)
                if n > 2:
                    dve.wait_ge(stored[u], 16 * (((n - 1) // 2) + k))
                nc.vector.tensor_tensor(result[:, u], kept[:, u], grown[:, u], ALU.add).then_inc(finished, 1)

            def body(ref, k):
                if ref + 2 < V:
                    own(ref + 2, k)
                if ref + 1 < V:
                    front(ref + 1, k)
                if ref < V:
                    back(ref, k)
                if ref >= 1 and VISITS[ref - 1].last:
                    end(ref - 1, k)
            own(0, 0)
            own(1, 0)
            front(0, 0)
            walk(dve, body)

        @block.tensor
        def _(pe):
            def look_up(ref, k):
                v, u, w = ref + 2 * k, ref % 2, VISITS[ref]
                pe.wait_ge(owners, v + 1)
                if ref >= 2:
                    pe.wait_ge(facts_done, v - 1)
                rows, info = looked(psC, u, w), info_of(ref, k)
                for q in range(w.blocks):
                    mm = nc.tensor.matmul(rows[:, q], owner[:, u, q * P:(q + 1) * P], info, start=True, stop=True)
                mm.then_inc(looked_up, 1)

            def gather_rows(ref, k):
                v, u, w = ref + 2 * k, ref % 2, VISITS[ref]
                n = tiles_ended(ref) if w.last else tiles_ended(ref) + 1
                o = (n - 1) % 2
                pe.wait_ge(weighted, v + 1)
                pe.wait_ge(to_row_done, v + 1)
                if n > 2 and w.first:
                    pe.wait_ge(agg_done, n - 2 + 2 * k)
                for q in range(w.blocks):
                    a, z = w.first and q == 0, w.last and q == w.blocks - 1
                    nc.tensor.matmul(psO[:, o], to_row[:, u, q], nodes[:, u, q, 0:HF], start=a, stop=z)
                    mm = nc.tensor.matmul(psD[:, o, 0:H], to_row[:, u, q], weight[:, u, q], start=a, stop=z)
                mm.then_inc(summed, 1)

            def body(ref, k):
                if ref + 2 < V:
                    look_up(ref + 2, k)
                if ref < V:
                    gather_rows(ref, k)
            look_up(0, 0)
            look_up(1, 0)
            walk(pe, body)


def lay_out_s2(nc, sb, s2_rows):
    BATCH = 4
    with ExitStack() as ctx:
        s2T = ctx.enter_context(nc.sbuf_tensor([H, N], F32))
        ps = ctx.enter_context(nc.psum_tensor([P, 2, 512], F32))
        transposed = ctx.enter_context(nc.semaphore())
        copied = ctx.enter_context(nc.semaphore())
        copied_odd = ctx.enter_context(nc.semaphore("copied_odd"))
        stored = ctx.enter_context(nc.semaphore())
        stored_too = ctx.enter_context(nc.semaphore("stored_too"))
        block = ctx.enter_context(nc.Block())

        @block.tensor
        def _(pe):
            for b in range(TILES // BATCH):
                if b >= 2:
                    pe.wait_ge(copied_odd if b % 2 else copied, b // 2)
                for j in range(BATCH):
                    mm = nc.tensor.transpose(ps[0:H, b % 2, j * P:(j + 1) * P], sb["s2"][:, b * BATCH + j], sb["ident"][:])
                mm.then_inc(transposed, 1)

        @block.vector
        def _(dve):
            for b in range(0, TILES // BATCH, 2):
                dve.wait_ge(transposed, b + 1)
                nc.vector.tensor_copy(s2T[:, b * 512:(b + 1) * 512], ps[0:H, 0]).then_inc(copied, 1)

        @block.scalar
        def _(act):
            for b in range(1, TILES // BATCH, 2):
                act.wait_ge(transposed, b + 1)
                nc.scalar.activation(s2T[:, b * 512:(b + 1) * 512], ps[0:H, 1], ACT.Copy).then_inc(copied_odd, 1)

        @block.sync
        def _(sp):
            sp.wait_ge(copied, TILES // BATCH // 2)
            sp.wait_ge(copied_odd, TILES // BATCH // 2)
            sp.dma_start(s2_rows[0:H // 2], s2T[0:H // 2]).then_inc(stored, 16)
            sp.wait_ge(stored, 16)

        @block.gpsimd
        def _(pool):
            pool.wait_ge(copied, TILES // BATCH // 2)
            pool.wait_ge(copied_odd, TILES // BATCH // 2)
            pool.dma_start(s2_rows[H // 2:H], s2T[H // 2:H]).then_inc(stored_too, 16)
            pool.wait_ge(stored_too, 16)


def dense_attention(nc, sb, x, adj, table, s2_rows, out):
    PAIR = 2
    PAIRS = H // PAIR
    BANKS = N // 512
    with ExitStack() as ctx:
        s2b = ctx.enter_context(nc.sbuf_tensor([P, PAIR, N], F32))
        h_pair = ctx.enter_context(nc.sbuf_tensor([P, TILES, PAIR * F], F32))
        adj_rows = ctx.enter_context(nc.sbuf_tensor([P, N], I32))
        barred = ctx.enter_context(nc.sbuf_tensor([P, N], F32))
        probs = ctx.enter_context(nc.sbuf_tensor([P, PAIR, N], F32))
        small = ctx.enter_context(nc.sbuf_tensor([P, PAIR, 4], F32))
        rowmax = ctx.enter_context(nc.sbuf_tensor([P, PAIR], F32))
        rowsum = ctx.enter_context(nc.sbuf_tensor([P, PAIR], F32))
        recip = ctx.enter_context(nc.sbuf_tensor([P, PAIR], F32))
        probsT = ctx.enter_context(nc.sbuf_tensor([P, 2, 512], F32))
        x_part = ctx.enter_context(nc.sbuf_tensor([P, PAIR * F], F32))
        fin = ctx.enter_context(nc.sbuf_tensor([P, 4, PAIR * F], F32))
        psT = ctx.enter_context(nc.psum_tensor([P, 2, 512], F32))
        psO = ctx.enter_context(nc.psum_tensor([P, 2, 512], F32))
        sem = lambda name: ctx.enter_context(nc.semaphore(name))
        pair_loaded, adj_loaded, x_loaded = sem("pair_loaded"), sem("adj_loaded"), sem("x_loaded")
        barred_done, scores_done = sem("barred_done"), sem("scores_done")
        max_part, max_done = sem("max_part"), sem("max_done")
        leaky_done, probs_done = sem("leaky_done"), sem("probs_done")
        transposed, probsT_done, summed_bank = sem("transposed"), sem("probsT_done"), sem("summed_bank")
        fin_part, fin_neg, fin_exp, fin_done = sem("fin_part"), sem("fin_neg"), sem("fin_exp"), sem("fin_done")
        stored = sem("stored")
        block = ctx.enter_context(nc.Block())
        adjt = adj.rearrange("(t p) n -> t p n", p=P)

        @block.sync
        def _(sp):
            sp.sem_inc(stored, 16)
            with sp.Fori(0, PAIRS) as g:
                sp.wait_ge(fin_done, g * TILES + 1)
                for u in range(PAIR):
                    sp.dma_start(s2b[:, u], broadcast_rows(s2_rows[bass.ds(g * PAIR + u, 1)][0])).then_inc(pair_loaded, 16)
                sp.dma_start(h_pair[:], table[0:N].rearrange("(t p) d -> p t d", p=P)[:, :, bass.ds(g * PAIR * F, PAIR * F)]
                             ).then_inc(pair_loaded, 16)
                with sp.Fori(0, TILES) as t:
                    step = g * TILES + t
                    sp.wait_ge(barred_done, step + 1)
                    sp.dma_start(adj_rows[:], adjt[bass.ds(t, 1)][0]).then_inc(adj_loaded, 16)
                    sp.wait_ge(fin_done, step + 1)
                    sp.dma_start(x_part[:], x.rearrange("(t p) d -> t p d", p=P)[bass.ds(t, 1)][0][:, bass.ds(g * PAIR * F, PAIR * F)]
                                 ).then_inc(x_loaded, 16)
                    sp.wait_ge(fin_done, step + 2)
                    sp.dma_start(out.rearrange("(t p) d -> t p d", p=P)[bass.ds(t, 1)][0][:, bass.ds(g * PAIR * F, PAIR * F)],
                                 fin[:, 3]).then_inc(stored, 16)
            sp.wait_ge(stored, 16 * PAIRS * TILES + 16)

        @block.vector
        def _(dve):
            for ahead in (fin_done, barred_done, scores_done, fin_neg):
                dve.sem_inc(ahead, 1)
            with dve.Fori(0, PAIRS) as g:
                with dve.Fori(0, TILES) as t:
                    step = g * TILES + t
                    dve.wait_ge(pair_loaded, 48 * g + 48)
                    dve.wait_ge(adj_loaded, 16 * step + 16)
                    dve.wait_ge(scores_done, 2 * step + 1)
                    nc.vector.tensor_scalar(barred[:], adj_rows[:], 0.0, NEG_BIG, ALU.is_le, ALU.mult).then_inc(barred_done, 1)
                    dve.wait_ge(barred_done, step + 2)
                    dve.wait_ge(summed_bank, 2 * BANKS * step + 1)
                    for u in range(PAIR):
                        s1 = sb["s1"][:, bass.ds(t, 1), bass.ds(g * PAIR + u, 1)].rearrange("p a b -> p (a b)")
                        nc.vector.scalar_tensor_tensor(probs[:, u], barred[:], s1, s2b[:, u], ALU.add, ALU.add).then_inc(scores_done, 1)
                        dve.wait_ge(scores_done, 2 * step + u + 2)
                        nc.vector.scalar_tensor_tensor(probs[:, u], probs[:, u], ALPHA, probs[:, u],
                                                       ALU.mult, ALU.max).then_inc(leaky_done, 1)
                        dve.wait_ge(leaky_done, 2 * step + u + 1)
                        nc.vector.tensor_reduce(small[:, u, 0:1], probs[:, u], AX.X, ALU.max).then_inc(max_part, 1)
                        dve.wait_ge(max_part, 2 * step + u + 1)
                        nc.vector.tensor_scalar(rowmax[:, u:u + 1], small[:, u, 0:1], -1.0, None, ALU.mult).then_inc(max_done, 1)
                    for u in range(PAIR):
                        for b in range(BANKS):
                            k = 2 * BANKS * step + u * BANKS + b
                            dve.wait_ge(transposed, k + 1)
                            if u * BANKS + b >= 2:
                                dve.wait_ge(summed_bank, k)
                            nc.vector.tensor_copy(probsT[:, b % 2], psT[:, b % 2]).then_inc(probsT_done, 1)
                    dve.wait_ge(probs_done, 2 * step + 2)
                    nc.vector.reciprocal(recip[:], rowsum[:]).then_inc(fin_part, 1)
                    dve.wait_ge(summed_bank, 2 * BANKS * step + 2 * BANKS + 1)
                    dve.wait_ge(fin_part, 3 * step + 1)
                    dve.wait_ge(stored, 16 * step + 16)
                    for u in range(PAIR):
                        nc.vector.tensor_scalar(fin[:, 0, u * F:(u + 1) * F], psO[:, u, 0:F], recip[:, u:u + 1], None,
                                                ALU.mult).then_inc(fin_part, 1)
                    dve.wait_ge(fin_part, 3 * step + 3)
                    nc.vector.tensor_scalar(fin[:, 1], fin[:, 0], 0.0, None, ALU.min).then_inc(fin_neg, 1)
                    dve.wait_ge(x_loaded, 16 * step + 16)
                    nc.vector.scalar_tensor_tensor(fin[:, 3], fin[:, 0], 0.0, x_part[:], ALU.max, ALU.add).then_inc(fin_neg, 1)
                    dve.wait_ge(fin_neg, 2 * step + 3)
                    dve.wait_ge(fin_exp, step + 1)
                    nc.vector.scalar_tensor_tensor(fin[:, 3], fin[:, 2], -1.0, fin[:, 3], ALU.add, ALU.add).then_inc(fin_done, 1)

        @block.scalar
        def _(act):
            with act.Fori(0, PAIRS) as g:
                with act.Fori(0, TILES) as t:
                    step = g * TILES + t
                    for u in range(PAIR):
                        act.wait_ge(max_done, 2 * step + u + 1)
                        nc.scalar.activation(probs[:, u], probs[:, u], ACT.Exp, bias=rowmax[:, u:u + 1],
                                             accum_out=rowsum[:, u:u + 1]).then_inc(probs_done, 1)
                    act.wait_ge(fin_neg, 2 * step + 2)
                    nc.scalar.activation(fin[:, 2], fin[:, 1], ACT.Exp).then_inc(fin_exp, 1)

        @block.tensor
        def _(pe):
            pe.sem_inc(summed_bank, 1)
            with pe.Fori(0, PAIRS) as g:
                with pe.Fori(0, TILES) as t:
                    step = g * TILES + t
                    pe.wait_ge(pair_loaded, 48 * g + 48)
                    pe.wait_ge(fin_neg, 2 * step + 1)
                    for u in range(PAIR):
                        pe.wait_ge(probs_done, 2 * step + u + 1)

                        def turn_bank(b):
                            k = 2 * BANKS * step + u * BANKS + b
                            if u * BANKS + b >= 2:
                                pe.wait_ge(probsT_done, k - 1)
                            for j in range(4):
                                mm = nc.tensor.transpose(psT[:, b % 2, j * P:(j + 1) * P],
                                                         probs[:, u, (4 * b + j) * P:(4 * b + j + 1) * P], sb["ident"][:])
                            mm.then_inc(transposed, 1)

                        def sum_bank(b):
                            k = 2 * BANKS * step + u * BANKS + b
                            pe.wait_ge(probsT_done, k + 1)
                            for j in range(4):
                                mm = nc.tensor.matmul(psO[:, u, 0:F], probsT[:, b % 2, j * P:(j + 1) * P],
                                                      h_pair[:, 4 * b + j, u * F:(u + 1) * F],
                                                      start=(b == 0 and j == 0), stop=(b == BANKS - 1 and j == 3))
                            mm.then_inc(summed_bank, 1)
                            return mm
                        turn_bank(0)
                        for b in range(BANKS):
                            if b + 1 < BANKS:
                                turn_bank(b + 1)
                            mm = sum_bank(b)


def build(nc, x, adj, W, a1, a2, out):
    table = nc.dram_tensor("table", (N + 1, TABLE), F32).ap()
    s2_rows = nc.dram_tensor("s2_rows", (H, N), F32).ap()
    with ExitStack() as ctx:
        def buf(name, shape, dtype=F32):
            return ctx.enter_context(nc.sbuf_tensor(name, shape, dtype))
        sb = {name: buf(name, shape) for name, shape in (("ident", [P, P]), ("ones", [P, P]), ("s1", [P, TILES, H]),
                                                         ("s2", [P, TILES, H]))}
        sb["flag"] = buf("flag", [1, 1], I32)
        with ExitStack() as edges:
            def tmp(name, shape, dtype=F32):
                sb[name] = edges.enter_context(nc.sbuf_tensor(name, shape, dtype))
            for kind in "ABC":
                tmp("info" + kind, [P, COUNT[kind], SLOTS[kind] + INFO])
            tmp("fullest", [P, V])
            tmp("neg_centre", [P, V])
            tmp("half_sq", [P, V])
            tmp("node_sum", [P, HF])
            with ExitStack() as scan:
                for name, shape, dtype in (("W", [P, KC, HF], F32), ("Wa", [P, KC, 2 * H], F32),
                                           ("step_diag", [P, P], BF16), ("radix", [2, P], BF16),
                                           ("digits", [2, N], BF16)):
                    sb[name] = scan.enter_context(nc.sbuf_tensor("sb_" + name, shape, dtype))
                setup(nc, sb, W, a1, a2)
                scan_constants(nc, sb)
                project_and_scan(nc, sb, x, adj, table)
            plan(nc, sb, table)
            attend_edges(nc, sb, x, table, out)
        flag = nc.values_load(sb["flag"][0:1, 0:1], min_val=0, max_val=1, skip_runtime_bounds_check_because="a comparison wrote it")
        with nc.If(flag > 0):
            lay_out_s2(nc, sb, s2_rows)
            dense_attention(nc, sb, x, adj, table, s2_rows, out)


_INS = ['x', 'adj', 'L0_gnn_W', 'L0_gnn_a1', 'L0_gnn_a2']
_OUTS = [((6144, 512), 'float32')]


def kernel(**inputs):
    import numpy as _np
    import concourse.bacc as _bacc
    from concourse import mybir as _mybir
    from concourse.bass_utils import run_bass_kernel_spmd as _run

    nc = _bacc.Bacc("TRN2", target_bir_lowering=False, num_devices=1)
    arrays, args = {}, []
    for name in _INS:
        a = _np.ascontiguousarray(inputs[name])
        arrays[f"in_{name}_dram"] = a
        args.append(nc.dram_tensor(f"in_{name}_dram", a.shape, _mybir.dt.from_np(a.dtype), kind="ExternalInput").ap())
    for i, (shape, dtype) in enumerate(_OUTS):
        dt = _mybir.dt.from_np(_np.dtype(dtype))
        args.append(nc.dram_tensor(f"out_{i}_dram", shape, dt, kind="ExternalOutput").ap())
    build(nc, *args)
    r = _run(nc, [arrays], core_ids=[0])
    got = tuple(r.results[0][f"out_{i}_dram"] for i in range(len(_OUTS)))
    return got[0]
```

```python
import concourse.bass as bass
from concourse import mybir
from contextlib import ExitStack

F32 = mybir.dt.float32
BF16 = mybir.dt.bfloat16
I32 = mybir.dt.int32
ALU = mybir.AluOpType
ACT = mybir.ActivationFunctionType
AX = mybir.AxisListType

P = 128
N = 6144
D = 512
H = 8
F = 64
HF = H * F
TILES = N // P
KC = D // P
TABLE = HF + H
EPS = 1e-5
ALPHA = 0.2
NEG_BIG = -9e15


FLAG_SPREAD = 60.0
STEP = 1 << 14
INFO = 2 + 2 * H
GROUP = 1024
GROUPS = N // GROUP


def cuts(shares, inside=(), narrowest=8):
    marks = {0, N} | set(range(0, N, 512)) | set(inside)
    marks |= {narrowest * round(N * (k / shares) ** 2 / narrowest) for k in range(1, shares)}
    marks = sorted(marks)
    kept = [0]
    for m in marks[1:]:
        if m - kept[-1] >= narrowest:
            kept.append(m)
    return list(zip(kept[:-1], kept[1:]))


class Visit:
    def __init__(self, tile, lo, hi, segments, slots, blocks, kind, place, first, last):
        self.tile, self.lo, self.hi, self.slots, self.blocks = tile, lo, hi, slots, blocks
        self.segments = [s for s in segments if lo <= s[0] < hi]
        self.kind, self.place, self.first, self.last = kind, place, first, last


def edge_blocks(tile):
    for start, blocks in ((38, 3), (18, 4), (12, 5), (8, 6), (6, 7), (4, 8), (2, 10)):
        if tile >= start:
            return blocks


def make_visits():
    visits = []
    eighths = [128 * round(N * (k / 8) ** 2 / 128) for k in range(9)]
    fine = cuts(96, eighths)
    for k in range(8):
        visits.append(Visit(0, eighths[k], eighths[k + 1], fine, 40, 4, "A", k, k == 0, k == 7))
    half = cuts(24)
    for k, (lo, hi) in enumerate(((0, 1536), (1536, N))):
        visits.append(Visit(1, lo, hi, half, 24, 7, "B", k, k == 0, k == 1))
    middle = cuts(1, (32, 128, 256))
    for t in range(2, 12):
        visits.append(Visit(t, 0, N, middle, 24, edge_blocks(t), "B", t, True, True))
    wide = [(0, 128), (128, 512), (512, 1024)] + [(g * GROUP, (g + 1) * GROUP) for g in range(1, GROUPS)]
    for t in range(12, TILES):
        visits.append(Visit(t, 0, N, wide, 16, edge_blocks(t), "C", t - 12, True, True))
    return visits


VISITS = make_visits()
V = len(VISITS)
SLOTS = {"A": 40, "B": 24, "C": 16}
SHARED = 4
COUNT = {"A": 8, "B": 12, "C": 36}
FIRST = {"A": 0, "B": 8, "C": 20}
SEGMENTS = max(len(v.segments) for v in VISITS)
BLOCKS = max(v.blocks for v in VISITS)


def at(count, ref, k):
    return count(ref) if isinstance(k, int) and k == 0 else count(ref) + k * (count(ref + 2) - count(ref))


def broadcast_rows(ap, rows=P):
    return bass.AP(tensor=ap.tensor, offset=ap.offset, ap=[[0, rows]] + list(ap.ap))


def S1(sb):
    return sb["s12"][:, 0]


def S2(sb):
    return sb["s12"][:, 1]


def setup(nc, sb, x, adj, W, a1, a2):
    with ExitStack() as ctx:
        a_rows = ctx.enter_context(nc.sbuf_tensor("a_rows", [P, 2, H, F], F32))
        product = ctx.enter_context(nc.sbuf_tensor("product", [P, 2, 2, H, F], F32))
        high = ctx.enter_context(nc.sbuf_tensor("high", [33, N // 256], F32))
        low = ctx.enter_context(nc.sbuf_tensor("low", [33, 256], F32))
        w_loaded, a_loaded, ones_set = (ctx.enter_context(nc.semaphore(n)) for n in ("w_loaded", "a_loaded", "ones_set"))
        product_done, folded, cleared = (ctx.enter_context(nc.semaphore(n)) for n in ("product_done", "folded", "cleared"))
        block = ctx.enter_context(nc.Block())

        @block.sync
        def _(sp):
            sp.dma_start(a_rows[:, 0], broadcast_rows(a1)).then_inc(a_loaded, 16)
            sp.dma_start(a_rows[:, 1], broadcast_rows(a2)).then_inc(a_loaded, 16)
            for kc in range(KC):
                sp.dma_start(sb["W"][:, kc, :].rearrange("p (h f) -> p h f", h=H),
                             W[:, kc * P:(kc + 1) * P, :].rearrange("h p f -> p h f")).then_inc(w_loaded, 16)
            for u in range(2):
                sp.dma_start(sb["x_rows"][:, u], x[u * P:(u + 1) * P]).then_inc(sb["x_loaded"][u], 16)
                sp.dma_start(sb["adj_rows"][:, u], adj[u * P:(u + 1) * P]).then_inc(sb["adj_loaded"][u], 16)

        @block.gpsimd
        def _(pool):
            nc.gpsimd.memset(sb["ones"][:], 1.0).then_inc(ones_set, 1)
            pool.wait_ge(ones_set, 1)
            nc.gpsimd.affine_select(out=sb["ident"][:], in_=sb["ones"][:], compare_op=ALU.is_equal, fill=0.0,
                                    base=0, pattern=[[-1, P]], channel_multiplier=1).then_inc(ones_set, 1)
            pool.wait_ge(cleared, 3)
            pool.wait_ge(ones_set, 2)
            nc.gpsimd.iota(high[0:1, :], [[-1, N // 256]], base=N // 256 - 1, channel_multiplier=0,
                           allow_small_or_imprecise_dtypes=True).then_inc(ones_set, 1)
            pool.wait_ge(ones_set, 3)
            nc.gpsimd.iota(low[32:33, :], [[-1, 256]], base=256, channel_multiplier=0,
                           allow_small_or_imprecise_dtypes=True).then_inc(ones_set, 1)

        def fold(dve, kc):
            dve.wait_ge(product_done, kc + 1)
            nc.vector.tensor_reduce(sb["Wa"][:, kc, :], product[:, kc % 2].rearrange("p a h f -> p (a h) f"),
                                    AX.X, ALU.add).then_inc(folded, 1)

        @block.vector
        def _(dve):
            nc.vector.memset(high[:], 0.0).then_inc(cleared, 1)
            nc.vector.memset(low[:], 0.0).then_inc(cleared, 1)
            nc.vector.memset(sb["radix"][:], 0.0).then_inc(cleared, 1)
            dve.wait_ge(cleared, 3)
            nc.vector.memset(sb["radix"][0:1, :], 256.0)
            nc.vector.memset(sb["radix"][32:33, :], 1.0)
            dve.wait_ge(ones_set, 4)
            nc.vector.tensor_tensor(sb["digits"][:].rearrange("p (a b) -> p a b", b=256),
                                    high[:].unsqueeze(2).to_broadcast([33, N // 256, 256]),
                                    low[:].unsqueeze(1).to_broadcast([33, N // 256, 256]), ALU.add)
            dve.wait_ge(ones_set, 2)
            nc.vector.tensor_scalar(sb["step_diag"][:], sb["ident"][:], float(STEP), None, ALU.mult)
            dve.wait_ge(a_loaded, 32)
            for kc in range(KC):
                dve.wait_ge(w_loaded, 16 * KC)
                if kc >= 2:
                    dve.wait_ge(folded, kc - 1)
                nc.vector.tensor_tensor(product[:, kc % 2], sb["W"][:, kc, :].rearrange("p (h f) -> p h f", h=H)
                                        .unsqueeze(1).to_broadcast([P, 2, H, F]), a_rows[:], ALU.mult).then_inc(product_done, 1)
                if kc >= 1:
                    fold(dve, kc - 1)
            fold(dve, KC - 1)


def project_and_scan(nc, sb, x, adj, table):
    HALF = TILES // 2
    PLAN = [("tile", t) for t in range(4)] + [("loop", 4, 12), ("tile", 12), ("tile", 13), ("loop", 14, TILES - 2),
                                              ("tile", TILES - 2), ("tile", TILES - 1)]
    of_tile = [[v for v in VISITS if v.tile == t] for t in range(TILES)]
    x_rows, adj_rows, x_loaded, adj_loaded = (sb[n] for n in ("x_rows", "adj_rows", "x_loaded", "adj_loaded"))
    with ExitStack() as ctx:
        def buf(name, shape, dtype=F32):
            return ctx.enter_context(nc.sbuf_tensor(name, shape, dtype))

        def psum(name, shape):
            return ctx.enter_context(nc.psum_tensor(name, shape, F32))

        def sem(name):
            return ctx.enter_context(nc.semaphore(name))
        stats = buf("stats", [P, 2, 6])
        both, gap = buf("both", [P, 2, 3]), buf("gap", [P, 2, 3])
        weight_of_gap, minus_half = buf("weight_of_gap", [P, 1]), buf("minus_half", [P, 1])
        squares, std, rstd, shift = (buf(n, [P, 2, 1]) for n in ("squares", "std", "rstd", "shift"))
        scaled, eps = buf("scaled", [P, 2, 1]), buf("eps", [P, 1])
        normed, normedT, h_rows = buf("normed", [P, 2, D]), buf("normedT", [P, 2, KC, P]), buf("h_rows", [P, 2, TABLE])
        adj_bf = buf("adj_bf", [P, 2, N], BF16)
        cands = buf("cands", [P, 2, SEGMENTS * 8])
        found = buf("found", [P, 2, max(SLOTS.values())])
        psK, psT = psum("psK", [P, 2, GROUP]), psum("psT", [P, KC, P])
        psH, psS = psum("psH", [P, 2, HF]), psum("psS", [P, 512])
        stored = [sem(f"stored{u}") for u in range(2)]
        stats_done, moment_step, squares_done, std_done = sem("stats_done"), sem("moment_step"), sem("squares_done"), sem("std_done")
        rstd_done, scaled_done, shift_done, norm_done = sem("rstd_done"), sem("scaled_done"), sem("shift_done"), sem("norm_done")
        transposed, normedT_done, projected = sem("transposed"), sem("normedT_done"), sem("projected")
        h_copied, added, consts_set = sem("h_copied"), sem("added"), sem("consts_set")
        adj_converted, keys_ready = sem("adj_converted"), sem("keys_ready")
        segments_done, cands_cut, slots_done, scan_turn = sem("segments_done"), sem("cands_cut"), sem("slots_done"), sem("scan_turn")
        key_turn = sem("key_turn")
        block = ctx.enter_context(nc.Block())
        xt = x.rearrange("(t p) d -> t p d", p=P)
        adjt = adj.rearrange("(t p) n -> t p n", p=P)
        tt = table[0:N].rearrange("(t p) d -> t p d", p=P)

        def tile_at(ap, t):
            return ap[t] if isinstance(t, int) else ap[bass.ds(t, 1)][0]

        def walk(eng, body, start=0):
            for kind, *span in PLAN[start:]:
                if kind == "tile":
                    body(span[0], 0)
                else:
                    with eng.Fori(0, (span[1] - span[0]) // 2) as k:
                        for u in range(2):
                            body(span[0] + u, k)

        def pairs(t):
            return 16 * (t // 2 + 1)

        def segs_before(t, group=0):
            return sum(len(v.segments) for v in VISITS if v.tile < t) + \
                sum(1 for v in of_tile[t] for s in v.segments if s[0] // GROUP < group)

        def cut_count(t):
            return sum(2 * (v.slots // 8) - 1 for v in VISITS if v.tile < t)

        def visit_count(t):
            return sum(1 for v in VISITS if v.tile < t)

        @block.sync
        def _(sp):
            def body(ref, k):
                t, u = ref + 2 * k, ref % 2
                if ref + 2 < TILES:
                    sp.wait_ge(adj_converted, GROUPS * (t + 1))
                    sp.dma_start(adj_rows[:, u], tile_at(adjt, t + 2)).then_inc(adj_loaded[u], 16)
                    sp.wait_ge(norm_done, t + 1)
                    sp.dma_start(x_rows[:, u], tile_at(xt, t + 2)).then_inc(x_loaded[u], 16)
                if ref >= 1:
                    sp.wait_ge(h_copied, t)
                    sp.dma_start(tile_at(tt, t - 1), h_rows[:, 1 - u]).then_inc(stored[1 - u], 16)
            walk(sp, body)
            sp.wait_ge(h_copied, TILES)
            sp.dma_start(tt[TILES - 1], h_rows[:, 1]).then_inc(stored[1], 16)
            for u in range(2):
                sp.wait_ge(stored[u], 16 * HALF)

        @block.vector
        def _(dve):
            def moments(ref, k):
                t, u = ref + 2 * k, ref % 2
                dve.wait_ge(x_loaded[u], at(pairs, ref, k))
                if ref >= 2:
                    dve.wait_ge(squares_done, t - 1)
                nc.vector.bn_stats(stats[:, u], x_rows[:, u]).then_inc(stats_done, 1)

            def scale(ref, k):
                t, u = ref + 2 * k, ref % 2
                dve.wait_ge(std_done, t + 1)
                if ref >= 2:
                    dve.wait_ge(norm_done, t - 1)
                nc.vector.reciprocal(rstd[:, u], std[:, u]).then_inc(rstd_done, 1)

            def buffer_of(ref, which):
                return (visit_count(ref) + which) % 2 if ref < 2 else ref % 2

            def fill(ref, k, which):
                u, v = buffer_of(ref, which), of_tile[ref][which]
                number = visit_count(ref) + which
                eighth = cands[:, u, 0:len(v.segments) * 8].rearrange("p (s e) -> p s e", e=8)[:, :, 7]
                cell = sb["fullest"][:, number:number + 1] if isinstance(k, int) else \
                    sb["fullest"][:, bass.ds(number + 2 * k, 1)]
                nc.vector.tensor_reduce(cell, eighth, AX.X, ALU.max)

            def rank(ref, k, which, cut, n):
                u, v = buffer_of(ref, which), of_tile[ref][which]
                width, r = len(v.segments) * 8, n // 2
                if n:
                    dve.wait_ge(cands_cut, at(cut_count, ref, k) + cut)
                    dve.sem_inc(scan_turn, 1)
                if n % 2 == 0:
                    nc.vector.max(found[:, u, 8 * r:8 * r + 8], cands[:, u, 0:width]).then_inc(cands_cut, 1)
                else:
                    nc.vector.match_replace(cands[:, u, 0:width], found[:, u, 8 * r:8 * r + 8], cands[:, u, 0:width],
                                            -1.0).then_inc(cands_cut, 1)

            def list_slots(ref, k, which, cut):
                u, v = buffer_of(ref, which), of_tile[ref][which]
                dve.wait_ge(cands_cut, at(cut_count, ref, k) + cut)
                info = sb["info" + v.kind]
                if isinstance(k, int):
                    dst = info[:, v.place, 0:v.slots]
                else:
                    dst = info[:, bass.ds(v.place + 2 * k, 1), 0:v.slots].rearrange("p a b -> p (a b)")
                nc.vector.tensor_scalar(dst, found[:, u, 0:v.slots], -float(STEP), 0.0, ALU.add, ALU.max).then_inc(slots_done, 1)

            def rank_light(ref, k, g):
                steps = 2 * (of_tile[ref][0].slots // 8) - 1
                if g == 0:
                    dve.wait_ge(segments_done, at(segs_before, ref, k) + len(of_tile[ref][0].segments))
                    fill(ref, k, 0)
                if g < steps:
                    rank(ref, k, 0, g, g)
                if g == GROUPS - 1:
                    list_slots(ref, k, 0, steps)

            def body(ref, k):
                t, u = ref + 2 * k, ref % 2
                if ref == 2:
                    scale(3, 0)
                elif ref + 1 < TILES:
                    moments(ref + 1, k)
                for g in range(GROUPS):
                    dve.wait_ge(keys_ready, GROUPS * t + g + 1)
                    dve.sem_inc(scan_turn, 1)
                    segments = of_tile[ref][0].segments
                    for j, (lo, hi) in enumerate(segments):
                        if lo // GROUP == g:
                            nc.vector.max(cands[:, u, 8 * j:8 * j + 8],
                                          psK[:, g % 2, lo - g * GROUP:hi - g * GROUP]).then_inc(segments_done, 1)
                    if ref >= 3:
                        rank_light(ref - 1, k, g)
                    if g == 3 and 2 < ref + 1 < TILES and ref != 2:
                        scale(ref + 1, k)

            def heavy(tile):
                shares = of_tile[tile]
                searches = [(which, j, lo, hi) for which, v in enumerate(shares) for j, (lo, hi) in enumerate(v.segments)]
                ends = [sum(len(v.segments) for v in shares[:which + 1]) for which in range(len(shares))]

                def search(n):
                    which, j, lo, hi = searches[n]
                    g = lo // GROUP
                    if n == 0 or searches[n - 1][2] // GROUP != g:
                        dve.wait_ge(keys_ready, GROUPS * tile + g + 1)
                        dve.sem_inc(scan_turn, 1)
                    nc.vector.max(cands[:, buffer_of(tile, which), 8 * j:8 * j + 8],
                                  psK[:, g % 2, lo - g * GROUP:hi - g * GROUP]).then_inc(segments_done, 1)

                for n in range(ends[0]):
                    search(n)
                cut = 0
                for which, v in enumerate(shares):
                    steps = 2 * (v.slots // 8) - 1
                    dve.wait_ge(segments_done, segs_before(tile) + ends[which])
                    fill(tile, 0, which)
                    begin, end = ends[which], ends[min(which + 1, len(shares) - 1)]
                    for n in range(steps):
                        rank(tile, 0, which, cut, n)
                        cut += 1
                        for m in range(begin + (end - begin) * n // steps, begin + (end - begin) * (n + 1) // steps):
                            search(m)
                    list_slots(tile, 0, which, cut)
                    if which == (0 if tile else len(shares) // 2):
                        moments(tile + 2, 0)
            moments(0, 0)
            scale(0, 0)
            moments(1, 0)
            for tile in range(2):
                scale(tile + 1, 0)
                heavy(tile)
            walk(dve, body, 2)
            for g in range(GROUPS):
                rank_light(TILES - 1, 0, g)

        @block.scalar
        def _(act):
            def convert(ref, k, g):
                t, u = ref + 2 * k, ref % 2
                if g == 0:
                    act.wait_ge(adj_loaded[u], at(pairs, ref, k))
                if ref >= 2:
                    act.wait_ge(keys_ready, GROUPS * (t - 2) + g + 1)
                nc.scalar.activation(adj_bf[:, u, g * GROUP:(g + 1) * GROUP], adj_rows[:, u, g * GROUP:(g + 1) * GROUP],
                                     ACT.Copy).then_inc(adj_converted, 1)

            def deviation(ref, k):
                t, u = ref + 2 * k, ref % 2
                act.wait_ge(squares_done, t + 1)
                if ref >= 2:
                    act.wait_ge(rstd_done, t - 1)
                nc.scalar.activation(std[:, u], squares[:, u], ACT.Sqrt, bias=eps[:], scale=1.0 / D).then_inc(std_done, 1)

            def norm(ref, k):
                t, u = ref + 2 * k, ref % 2
                act.wait_ge(shift_done, t + 1)
                if ref >= 2:
                    act.wait_ge(transposed, t - 1)
                nc.scalar.activation(normed[:, u], x_rows[:, u], ACT.Relu, bias=shift[:, u],
                                     scale=rstd[:, u]).then_inc(norm_done, 1)

            def h_out(ref, k):
                t, u = ref + 2 * k, ref % 2
                act.wait_ge(projected, t + 1)
                if ref >= 2:
                    act.wait_ge(stored[u], at(pairs, ref - 2, k))
                    act.wait_ge(added, t - 1)
                nc.scalar.activation(h_rows[:, u, 0:HF], psH[:, u], ACT.Copy)
                if isinstance(k, int):
                    scores = sb["s12"][:, :, t]
                else:
                    scores = sb["s12"][:, :, bass.ds(t, 1)].rearrange("p a b h -> p a (b h)")
                nc.scalar.activation(scores, psS[:, 0:2 * H].rearrange("p (a h) -> p a h", a=2), ACT.Copy)
                nc.scalar.activation(h_rows[:, u, HF:TABLE], psS[:, H:2 * H], ACT.Copy).then_inc(h_copied, 1)

            def body(ref, k):
                t, u = ref + 2 * k, ref % 2
                act.wait_ge(transposed, t + 1)
                if ref >= 2:
                    act.wait_ge(projected, t - 1)
                nc.scalar.activation(normedT[:, u], psT[:], ACT.Copy).then_inc(normedT_done, 1)
                more = ref + 1 < TILES
                if ref in (0, 2):
                    deviation(ref + 1, 0)
                if more:
                    convert(ref + 1, k, 0)
                    convert(ref + 1, k, 1)
                if ref >= 1:
                    h_out(ref - 1, k)
                if more:
                    convert(ref + 1, k, 2)
                    if ref not in (0, 2):
                        deviation(ref + 1, k)
                    convert(ref + 1, k, 3)
                    convert(ref + 1, k, 4)
                    norm(ref + 1, k)
                    convert(ref + 1, k, 5)
            act.wait_ge(consts_set, 4)
            deviation(0, 0)
            for g in range(GROUPS):
                convert(0, 0, g)
            norm(0, 0)
            walk(act, body)
            h_out(TILES - 1, 0)

        @block.tensor
        def _(pe):
            def keys(ref, k, g):
                t, u = ref + 2 * k, ref % 2
                pe.wait_ge(adj_converted, GROUPS * t + g + 1)
                if g >= 2:
                    pe.wait_ge(segments_done, at(lambda n: segs_before(n, g - 1), ref, k))
                elif ref >= 1:
                    pe.wait_ge(segments_done, at(lambda n: segs_before(n - 1, GROUPS - 1 + g), ref, k))
                pe.sem_inc(key_turn, 1)
                for b in range(GROUP // 512):
                    c = g * GROUP + b * 512
                    nc.tensor.matmul(psK[:, g % 2, b * 512:(b + 1) * 512], sb["step_diag"][:], adj_bf[:, u, c:c + 512],
                                     start=True, stop=False)
                    mm = nc.tensor.matmul(psK[:, g % 2, b * 512:(b + 1) * 512], sb["radix"][:], sb["digits"][:, c:c + 512],
                                          start=False, stop=True)
                mm.then_inc(keys_ready, 1)

            def turn(ref, k):
                t, u = ref + 2 * k, ref % 2
                pe.wait_ge(norm_done, t + 1)
                if ref >= 1:
                    pe.wait_ge(normedT_done, t)
                for kc in range(KC):
                    mm = nc.tensor.transpose(psT[:, kc], normed[:, u, kc * P:(kc + 1) * P], sb["ident"][:])
                mm.then_inc(transposed, 1)

            def project_slice(ref, k, kc):
                t, u = ref + 2 * k, ref % 2
                if kc == 0:
                    pe.wait_ge(normedT_done, t + 1)
                    if ref >= 1:
                        pe.wait_ge(h_copied, t)
                nc.tensor.matmul(psH[:, u], normedT[:, u, kc], sb["W"][:, kc], start=(kc == 0), stop=(kc == KC - 1))
                mm = nc.tensor.matmul(psS[:, 0:2 * H], normedT[:, u, kc], sb["Wa"][:, kc],
                                      start=(kc == 0), stop=(kc == KC - 1))
                if kc == KC - 1:
                    mm.then_inc(projected, 1)

            def body(ref, k):
                turn(ref, k)
                for g in range(GROUPS):
                    keys(ref, k, g)
                    if g >= GROUPS - KC:
                        project_slice(ref, k, g - (GROUPS - KC))
            walk(pe, body)

        @block.gpsimd
        def _(pool):
            nc.gpsimd.memset(weight_of_gap[:], D / 4.0).then_inc(consts_set, 1)
            nc.gpsimd.memset(minus_half[:], -0.5).then_inc(consts_set, 1)
            nc.gpsimd.memset(eps[:], EPS).then_inc(consts_set, 1)
            nc.gpsimd.memset(sb["node_sum"][:], 0.0).then_inc(consts_set, 1)
            pool.wait_ge(consts_set, 4)

            def spread(ref, k):
                t, u = ref + 2 * k, ref % 2
                pool.wait_ge(stats_done, t + 1)
                if ref >= 2:
                    pool.wait_ge(std_done, t - 1)
                nc.gpsimd.tensor_tensor(both[:, u], stats[:, u, 0:3], stats[:, u, 3:6], ALU.add).then_inc(moment_step, 1)
                nc.gpsimd.tensor_tensor(gap[:, u, 0:1], stats[:, u, 4:5], stats[:, u, 1:2], ALU.subtract).then_inc(moment_step, 1)
                pool.wait_ge(moment_step, 4 * t + 2)
                nc.gpsimd.tensor_tensor(gap[:, u, 1:2], gap[:, u, 0:1], gap[:, u, 0:1], ALU.mult).then_inc(moment_step, 1)
                pool.wait_ge(moment_step, 4 * t + 3)
                nc.gpsimd.tensor_tensor(gap[:, u, 2:3], gap[:, u, 1:2], weight_of_gap[:], ALU.mult).then_inc(moment_step, 1)
                pool.wait_ge(moment_step, 4 * t + 4)
                nc.gpsimd.tensor_tensor(squares[:, u], both[:, u, 2:3], gap[:, u, 2:3], ALU.add).then_inc(squares_done, 1)

            def offset(ref, k):
                t, u = ref + 2 * k, ref % 2
                pool.wait_ge(rstd_done, t + 1)
                nc.gpsimd.tensor_tensor(scaled[:, u], both[:, u, 1:2], rstd[:, u], ALU.mult).then_inc(scaled_done, 1)
                pool.wait_ge(scaled_done, t + 1)
                if ref >= 2:
                    pool.wait_ge(norm_done, t - 1)
                nc.gpsimd.tensor_tensor(shift[:, u], scaled[:, u], minus_half[:], ALU.mult).then_inc(shift_done, 1)

            def add_up(ref, k):
                t, u = ref + 2 * k, ref % 2
                pool.wait_ge(h_copied, t + 1)
                if ref >= 1:
                    pool.wait_ge(added, t)
                nc.gpsimd.tensor_tensor(sb["node_sum"][:], sb["node_sum"][:], h_rows[:, u, 0:HF], ALU.add).then_inc(added, 1)

            def body(ref, k):
                if ref + 1 < TILES:
                    spread(ref + 1, k)
                if ref >= 1:
                    add_up(ref - 1, k)
                if ref + 1 < TILES:
                    offset(ref + 1, k)
            spread(0, 0)
            offset(0, 0)
            walk(pool, body)
            add_up(TILES - 1, 0)


def plan(nc, sb, table):
    with ExitStack() as ctx:
        def buf(name, shape, dtype=F32):
            return ctx.enter_context(nc.sbuf_tensor(name, shape, dtype))

        def sem(name):
            return ctx.enter_context(nc.semaphore(name))
        used = {kind: buf("used" + kind, [P, COUNT[kind], SLOTS[kind]]) for kind in "ABC"}
        degree, total, half = buf("degree", [P, V]), buf("total", [P, 2]), buf("half", [P, V])
        earlier, row_no = buf("earlier", [P, P]), buf("row_no", [P, 1])
        most, hi_lo, ext = buf("most", [P, 2 * H]), buf("hi_lo", [H, 2]), buf("ext", [H, 2 * H])
        bound8, spread = buf("bound8", [P, 2 * H]), buf("spread", [P, H])
        raw, bound = buf("raw", [P, TILES, H]), buf("bound", [P, TILES, H])
        flags, worst = buf("flags", [P, 4 * V + H]), buf("worst", [P, 1])
        mean_row, flag_f = buf("mean_row", [1, TABLE]), buf("flag_f", [1, 1])
        psA = ctx.enter_context(nc.psum_tensor("psA", [P, 512], F32))
        psB = ctx.enter_context(nc.psum_tensor("psB", [P, 512], F32))
        psC = ctx.enter_context(nc.psum_tensor("psC2", [P, 512], F32))
        psD = ctx.enter_context(nc.psum_tensor("psD2", [P, 512], F32))
        made, step, summed, stored = sem("made"), sem("step"), sem("summed"), sem("mean_stored")
        degrees_ready, extremes_ready = sem("degrees_ready"), sem("extremes_ready")
        worst_ready, mean_ready = sem("worst_ready"), sem("mean_ready")
        block = ctx.enter_context(nc.Block())

        @block.gpsimd
        def _(pool):
            nc.gpsimd.affine_select(out=earlier[:], in_=sb["ones"][:], compare_op=ALU.is_gt, fill=0.0,
                                    base=0, pattern=[[1, P]], channel_multiplier=-1).then_inc(made, 1)
            nc.gpsimd.iota(row_no[:], [[0, 1]], base=1, channel_multiplier=1, allow_small_or_imprecise_dtypes=True).then_inc(made, 1)

        @block.vector
        def _(dve):
            n = [0]

            def did(ins):
                n[0] += 1
                ins.then_inc(step, 1)

            def settle():
                dve.wait_ge(step, n[0])
            for kind in "ABC":
                did(nc.vector.tensor_scalar(used[kind][:], sb["info" + kind][:, :, 0:SLOTS[kind]], 0.0, None, ALU.is_gt))
            did(nc.vector.tensor_reduce(most[:, 0:H], S2(sb).rearrange("p t h -> p h t"), AX.X, ALU.max))
            did(nc.vector.tensor_reduce(most[:, H:2 * H], S2(sb).rearrange("p t h -> p h t"), AX.X, ALU.min))
            settle()
            for kind in "ABC":
                f, c = FIRST[kind], COUNT[kind]
                did(nc.vector.tensor_reduce(degree[:, f:f + c], used[kind][:], AX.X, ALU.add))
            settle()
            did(nc.vector.tensor_reduce(total[:, 0:1], degree[:, 0:8], AX.X, ALU.add))
            did(nc.vector.tensor_reduce(total[:, 1:2], degree[:, 8:10], AX.X, ALU.add))
            settle()
            did(nc.vector.scalar_tensor_tensor(degree[:, 0:1], total[:, 0:1], 0.0, degree[:, 0:1], ALU.is_equal, ALU.add))
            did(nc.vector.scalar_tensor_tensor(degree[:, 8:9], total[:, 1:2], 0.0, degree[:, 8:9], ALU.is_equal, ALU.add))
            did(nc.vector.scalar_tensor_tensor(degree[:, 10:V], degree[:, 10:V], 0.0, degree[:, 10:V], ALU.is_equal, ALU.add))
            settle()
            dve.sem_inc(degrees_ready, 1)
            dve.wait_ge(summed, 1)
            did(nc.vector.tensor_reduce(hi_lo[:, 0:1], psC[0:H, 0:P], AX.X, ALU.max))
            did(nc.vector.tensor_reduce(hi_lo[:, 1:2], psC[0:H, P:2 * P], AX.X, ALU.min))
            settle()
            did(nc.vector.tensor_scalar(ext[:, 0:H], sb["ident"][0:H, 0:H], hi_lo[:, 0:1], None, ALU.mult))
            did(nc.vector.tensor_scalar(ext[:, H:2 * H], sb["ident"][0:H, 0:H], hi_lo[:, 1:2], None, ALU.mult))
            settle()
            dve.sem_inc(extremes_ready, 1)
            dve.wait_ge(summed, 2)
            did(nc.vector.tensor_scalar(half[:], degree[:], 0.5, None, ALU.mult))
            settle()
            did(nc.vector.tensor_tensor(sb["half_sq"][:], half[:], half[:], ALU.mult))
            did(nc.vector.scalar_tensor_tensor(sb["neg_centre"][:], psA[:, 0:V], 1.0, half[:], ALU.mult, ALU.add))
            settle()
            did(nc.vector.tensor_scalar(sb["neg_centre"][:], sb["neg_centre"][:], -1.0, 0.5, ALU.mult, ALU.add))
            dve.wait_ge(summed, 3)
            did(nc.vector.tensor_copy(bound8[:], psD[:, 0:2 * H]))
            settle()
            did(nc.vector.tensor_tensor(raw[:], S1(sb), bound8[:, 0:H].unsqueeze(1).to_broadcast([P, TILES, H]), ALU.add))
            did(nc.vector.tensor_tensor(spread[:], bound8[:, 0:H], bound8[:, H:2 * H], ALU.subtract))
            settle()
            did(nc.vector.scalar_tensor_tensor(bound[:].rearrange("p t h -> p (t h)"), raw[:].rearrange("p t h -> p (t h)"), ALPHA,
                                               raw[:].rearrange("p t h -> p (t h)"), ALU.mult, ALU.max))
            dve.wait_ge(made, 2)
            settle()
            for kind in "ABC":
                f, c, s = FIRST[kind], COUNT[kind], SLOTS[kind]
                info = sb["info" + kind]
                did(nc.vector.tensor_copy(info[:, :, s:s + 1], psA[:, f:f + c].unsqueeze(2)))
                did(nc.vector.tensor_copy(info[:, :, s + 1:s + 2], row_no[:].unsqueeze(2).to_broadcast([P, c, 1])))
                shares = {"A": [(0, 8, 0, 1)], "B": [(0, 2, 1, 1), (2, 12, 2, 10)], "C": [(0, 36, 12, 36)]}[kind]
                for p0, p1, t0, nt in shares:
                    for src, o in ((S1(sb), 2), (bound, 2 + H)):
                        part = src[:, t0:t0 + nt]
                        if nt != p1 - p0:
                            part = part.to_broadcast([P, p1 - p0, H])
                        did(nc.vector.tensor_copy(info[:, p0:p1, s + o:s + o + H], part))
                did(nc.vector.tensor_scalar(flags[:, f:f + c], info[:, :, s - 1], 0.0, None, ALU.is_gt))
                did(nc.vector.tensor_scalar(flags[:, V + f:V + f + c], info[:, :, 0], STEP / 2.0, None, ALU.is_gt))
            did(nc.vector.tensor_scalar(flags[:, 2 * V:3 * V], sb["fullest"][:], float(STEP), None, ALU.is_ge))
            v0 = 0
            while v0 < V:
                v1 = v0
                while v1 < V and VISITS[v1].blocks == VISITS[v0].blocks:
                    v1 += 1
                did(nc.vector.tensor_scalar(flags[:, 3 * V + v0:3 * V + v1], psB[:, v0:v1], float(P * VISITS[v0].blocks), None, ALU.is_gt))
                v0 = v1
            did(nc.vector.tensor_scalar(flags[:, 4 * V:], spread[:], FLAG_SPREAD, None, ALU.is_gt))
            settle()
            did(nc.vector.tensor_reduce(worst[:], flags[:], AX.X, ALU.max))
            settle()
            dve.sem_inc(worst_ready, 1)
            dve.wait_ge(summed, 4)
            did(nc.vector.tensor_scalar(mean_row[:, 0:HF], psC[0:1, 0:HF], 1.0 / N, None, ALU.mult))
            did(nc.vector.tensor_copy(mean_row[:, HF:TABLE], bound8[0:1, 0:H]))
            settle()
            dve.sem_inc(mean_ready, 1)
            dve.wait_ge(summed, 5)
            did(nc.vector.tensor_scalar(flag_f[:], psA[0:1, 0:1], 0.0, None, ALU.is_gt))
            settle()
            nc.vector.tensor_copy(sb["flag"][:], flag_f[:]).then_inc(step, 1)

        @block.tensor
        def _(pe):
            pe.wait_ge(degrees_ready, 1)
            nc.tensor.transpose(psC[0:H, 0:P], most[:, 0:H], sb["ident"][:])
            nc.tensor.transpose(psC[0:H, P:2 * P], most[:, H:2 * H], sb["ident"][:]).then_inc(summed, 1)
            pe.wait_ge(made, 1)
            nc.tensor.matmul(psA[:, 0:V], earlier[:], degree[:], start=True, stop=True)
            nc.tensor.matmul(psB[:, 0:V], sb["ones"][:], degree[:], start=True, stop=True).then_inc(summed, 1)
            pe.wait_ge(extremes_ready, 1)
            nc.tensor.matmul(psD[:, 0:2 * H], sb["ones"][0:H, :], ext[:], start=True, stop=True).then_inc(summed, 1)
            nc.tensor.matmul(psC[:, 0:HF], sb["ones"][:], sb["node_sum"][:], start=True, stop=True).then_inc(summed, 1)
            pe.wait_ge(worst_ready, 1)
            nc.tensor.matmul(psA[0:1, 0:1], worst[:], sb["ones"][:, 0:1], start=True, stop=True).then_inc(summed, 1)

        @block.sync
        def _(sp):
            sp.wait_ge(mean_ready, 1)
            sp.dma_start(table[N:N + 1], mean_row[:]).then_inc(stored, 16)
            sp.wait_ge(stored, 16)


def attend_edges(nc, sb, x, table, out):
    with ExitStack() as ctx:
        def buf(name, shape, dtype=F32):
            return ctx.enter_context(nc.sbuf_tensor(name, shape, dtype))

        def psum(name, shape):
            return ctx.enter_context(nc.psum_tensor(name, shape, F32))

        def sem(name):
            return ctx.enter_context(nc.semaphore(name))
        edge_no = buf("edge_no", [P, BLOCKS * P])
        list_no = buf("list_no", [P, BLOCKS])
        distance, owner = buf("distance", [P, 2, BLOCKS * P]), buf("owner", [P, 2, BLOCKS * P])
        facts = buf("facts", [P, 2, 512])
        slot = buf("slot", [P, BLOCKS])
        chosen = buf("chosen", [P, BLOCKS * 24])
        key, column = buf("key", [P, BLOCKS]), buf("column", [P, 2, BLOCKS], mybir.dt.uint32)
        nodes = buf("nodes", [P, 2, BLOCKS, TABLE])
        weighted_h = buf("weighted_h", [P, 2, BLOCKS, HF])
        to_row = buf("to_row", [P, 2, BLOCKS, P])
        score, weight = buf("score", [P, 3, BLOCKS, H]), buf("weight", [P, 2, BLOCKS, H])
        recip, agg, below = buf("recip", [P, H]), buf("agg", [P, 2, HF]), buf("below", [P, HF])
        x_part, grown, kept, result = (buf(n, [P, 2, HF]) for n in ("x_part", "grown", "kept", "result"))
        psC, psO, psD = psum("psC", [P, 2, 512]), psum("psO", [P, 2, HF]), psum("psD", [P, 2, 512])
        psR = psum("psR", [P, 2, 512])
        gathered, x_loaded, stored = ([sem(f"{n}{u}") for u in range(2)] for n in ("gathered", "xe_loaded", "out_stored"))
        made = sem("counted")
        squared, owners, looked_up, facts_done = sem("squared"), sem("owners"), sem("looked_up"), sem("facts_done")
        front_step, columns, back_step, shifted = sem("front_step"), sem("columns"), sem("back_step"), sem("shifted")
        to_row_done, weights, weighted, summed = sem("to_row_done"), sem("weights"), sem("weighted"), sem("rows_summed")
        below_done, agg_done, grown_done, finished = sem("below_done"), sem("agg_done"), sem("grown_done"), sem("finished")
        act_turn, pool_turn, recips, kept_done = sem("act_turn"), sem("pool_turn"), sem("recips"), sem("kept_done")
        owners_turned, weighted_too = sem("owners_turned"), sem("weighted_too")
        block = ctx.enter_context(nc.Block())
        xt = x.rearrange("(t p) d -> t p d", p=P)
        ot = out.rearrange("(t p) d -> t p d", p=P)

        def tile_at(ap, t):
            return ap[t] if isinstance(t, int) else ap[bass.ds(t, 1)][0]

        def same(a, b):
            return VISITS[a].blocks == VISITS[b].blocks and VISITS[a].kind == VISITS[b].kind

        def walk(eng, body):
            v = 0
            while v <= V:
                end = v
                if v % 2 == 0 and v >= 12:
                    while end + 4 < V and same(v - 1, end) and same(v - 1, end + 4) and same(v - 1, v + 2):
                        end += 2
                if end > v + 2:
                    with eng.Fori(0, (end - v) // 2) as k:
                        for u in range(2):
                            body(v + u, k)
                    v = end
                else:
                    body(v, 0)
                    v += 1

        def one(v):
            return v + 1

        def tiles_ended(v):
            return sum(1 for w in VISITS[:v + 1] if w.last) if v < V else tiles_ended(V - 1) + v - V + 1

        def landed(v):
            return 16 * sum(w.blocks for w in VISITS[v % 2:v + 1:2])

        def shared(v):
            return VISITS[v].blocks <= SHARED

        def shares(v):
            return sum(shared(w) for w in range(v + 1))

        def looked(array, u, w):
            width = w.slots + INFO
            return array[:, u, 0:w.blocks * width].rearrange("p (q c) -> p q c", c=width)

        def by_head(array, u, lo, hi):
            return array[:, u, lo:hi, 0:HF].rearrange("p q (h f) -> p q h f", h=H)

        def turns(v):
            return sum(-(-w.blocks // 4) for w in VISITS[:v + 1])

        def info_of(ref, k):
            v = VISITS[ref]
            info = sb["info" + v.kind]
            if isinstance(k, int):
                return info[:, v.place]
            return info[:, bass.ds(v.place + 2 * k, 1)].rearrange("p a b -> p (a b)")

        def column_of(array, ref, k):
            return array[:, ref:ref + 1] if isinstance(k, int) else array[:, bass.ds(ref + 2 * k, 1)]

        @block.gpsimd
        def _(pool):
            nc.gpsimd.iota(edge_no[:], [[1, BLOCKS * P]], base=0, channel_multiplier=0, allow_small_or_imprecise_dtypes=True).then_inc(made, 1)
            nc.gpsimd.iota(list_no[:], [[P, BLOCKS]], base=0, channel_multiplier=1, allow_small_or_imprecise_dtypes=True).then_inc(made, 1)

            def gather(ref, k):
                v, u = ref + 2 * k, ref % 2
                pool.wait_ge(columns, v + 1)
                if ref >= 2:
                    pool.wait_ge(weighted, v - 1)
                    if shares(ref - 2):
                        pool.wait_ge(weighted_too, at(shares, ref - 2, k))
                pool.sem_inc(pool_turn, 1)
                for q in range(VISITS[ref].blocks):
                    nc.gpsimd.indirect_dma_start(out=nodes[:, u, q], out_offset=None, in_=table,
                                                 in_offset=bass.IndirectOffsetOnAxis(ap=column[:, u, q:q + 1], axis=0)
                                                 ).then_inc(gathered[u], 16)

            gather(0, 0)
            gather(1, 0)

            def body(ref, k):
                if ref < V and shared(ref):
                    v, u, q = ref + 2 * k, ref % 2, VISITS[ref].blocks
                    pool.wait_ge(weights, v + 1)
                    if ref >= 2:
                        pool.wait_ge(summed, v - 1)
                    nc.gpsimd.tensor_tensor(by_head(weighted_h, u, q - 1, q).rearrange("p q h f -> p (q h) f"),
                                            by_head(nodes, u, q - 1, q).rearrange("p q h f -> p (q h) f"),
                                            weight[:, u, q - 1].unsqueeze(2).to_broadcast([P, H, F]),
                                            ALU.mult).then_inc(weighted_too, 1)
                if ref + 2 < V:
                    gather(ref + 2, k)
            walk(pool, body)

        @block.sync
        def _(sp):
            def body(ref, k):
                if ref < V and VISITS[ref].last:
                    n = tiles_ended(ref)
                    u = (n - 1) % 2
                    t = n - 1 + 2 * k
                    if n > 2:
                        sp.wait_ge(finished, t - 1)
                    sp.dma_start(x_part[:, u], tile_at(xt, t)).then_inc(x_loaded[u], 16)
                if ref >= 2 and VISITS[ref - 2].last:
                    n = tiles_ended(ref - 2)
                    u = (n - 1) % 2
                    t = n - 1 + 2 * k
                    sp.wait_ge(finished, t + 1)
                    sp.dma_start(tile_at(ot, t), result[:, u]).then_inc(stored[u], 16)
            walk(sp, body)
            body(V + 1, 0)
            for u in range(2):
                sp.wait_ge(stored[u], 16 * (TILES // 2))

        @block.scalar
        def _(act):
            act.wait_ge(made, 1)

            def square(ref, k):
                v, u, q = ref + 2 * k, ref % 2, VISITS[ref].blocks
                if ref >= 2:
                    act.wait_ge(owners, v - 1)
                act.sem_inc(act_turn, 1)
                nc.scalar.activation(distance[:, u, 0:q * P], edge_no[:, 0:q * P], ACT.Square,
                                     bias=column_of(sb["neg_centre"], ref, k)).then_inc(squared, 1)

            def rows_out(ref, k):
                v, u, q = ref + 2 * k, ref % 2, VISITS[ref].blocks
                for b in range(0, q, 4):
                    n = min(4, q - b)
                    count = turns(ref - 1) + b // 4
                    step = 0 if isinstance(k, int) else k * (turns(ref + 1) - turns(ref - 1))
                    act.wait_ge(owners_turned, count + 1 + step)
                    if ref >= 2:
                        act.wait_ge(summed, v - 1)
                    nc.scalar.activation(to_row[:, u, b:b + n].rearrange("p a b -> p (a b)"), psR[:, count % 2, 0:n * P],
                                         ACT.Copy).then_inc(to_row_done, 1)

            def facts_out(ref, k):
                v, u, w = ref + 2 * k, ref % 2, VISITS[ref]
                act.wait_ge(looked_up, v + 1)
                if ref >= 2:
                    act.wait_ge(shifted, v - 1)
                nc.scalar.activation(looked(facts, u, w), looked(psC, u, w), ACT.Copy).then_inc(facts_done, 1)

            def body(ref, k):
                v, u = ref + 2 * k, ref % 2
                if ref < V:
                    q = VISITS[ref].blocks
                    rows_out(ref, k)
                    act.wait_ge(shifted, v + 1)
                    if ref >= 2:
                        act.wait_ge(summed, v - 1)
                    nc.scalar.activation(weight[:, u, 0:q], score[:, 2, 0:q], ACT.Exp).then_inc(weights, 1)
                if ref + 3 < V:
                    square(ref + 3, k)
                if ref + 2 < V:
                    facts_out(ref + 2, k)
                if ref >= 1 and VISITS[ref - 1].last:
                    n = tiles_ended(ref - 1)
                    t = n - 1 + 2 * k
                    act.wait_ge(agg_done, t + 1)
                    nc.scalar.activation(below[:], agg[:, (n - 1) % 2], ACT.Relu, scale=-1.0).then_inc(below_done, 1)
                    act.wait_ge(below_done, t + 1)
                    nc.scalar.activation(grown[:, (n - 1) % 2], below[:], ACT.Exp, scale=-1.0).then_inc(grown_done, 1)
            square(0, 0)
            square(1, 0)
            facts_out(0, 0)
            facts_out(1, 0)
            square(2, 0)
            walk(act, body)

        @block.vector
        def _(dve):
            dve.wait_ge(made, 2)

            def own(ref, k):
                v, u, q = ref + 2 * k, ref % 2, VISITS[ref].blocks
                dve.wait_ge(squared, v + 1)
                if ref >= 2:
                    dve.wait_ge(owners_turned, at(turns, ref - 2, k))
                nc.vector.tensor_scalar(owner[:, u, 0:q * P], distance[:, u, 0:q * P], column_of(sb["half_sq"], ref, k),
                                        None, ALU.is_lt).then_inc(owners, 1)

            def front(ref, k, n):
                v, u = ref + 2 * k, ref % 2
                w = VISITS[ref]
                q, s = w.blocks, w.slots
                rows = looked(facts, u, w)
                pick = chosen[:, 0:q * s].rearrange("p (q s) -> p q s", s=s)
                if n == 0:
                    dve.wait_ge(facts_done, v + 1)
                    nc.vector.tensor_tensor(slot[:, 0:q], list_no[:, 0:q], rows[:, :, s], ALU.subtract).then_inc(front_step, 1)
                elif n == 1:
                    dve.wait_ge(front_step, 4 * v + 1)
                    nc.vector.tensor_tensor(pick, edge_no[:, 0:s].unsqueeze(1).to_broadcast([P, q, s]),
                                            slot[:, 0:q].unsqueeze(2).to_broadcast([P, q, s]), ALU.is_equal).then_inc(front_step, 1)
                elif n == 2:
                    dve.wait_ge(front_step, 4 * v + 2)
                    nc.vector.tensor_tensor(pick, pick, rows[:, :, 0:s], ALU.mult).then_inc(front_step, 1)
                elif n == 3:
                    dve.wait_ge(front_step, 4 * v + 3)
                    nc.vector.tensor_reduce(key[:, 0:q], pick, AX.X, ALU.add).then_inc(front_step, 1)
                else:
                    dve.wait_ge(front_step, 4 * v + 4)
                    if ref >= 2:
                        dve.wait_ge(gathered[u], at(landed, ref - 2, k))
                    nc.vector.tensor_scalar(column[:, u, 0:q], key[:, 0:q], -1.0, float(N), ALU.mult, ALU.add).then_inc(columns, 1)

            def score_edges(ref, k, n):
                v, u, q, s = ref + 2 * k, ref % 2, VISITS[ref].blocks, VISITS[ref].slots
                rows = looked(facts, u, VISITS[ref])
                if n == 0:
                    dve.wait_ge(gathered[u], at(landed, ref, k))
                    nc.vector.tensor_tensor(score[:, 0, 0:q], nodes[:, u, 0:q, HF:TABLE], rows[:, :, s + 2:s + 2 + H],
                                            ALU.add).then_inc(back_step, 1)
                elif n == 1:
                    dve.wait_ge(back_step, 2 * v + 1)
                    nc.vector.scalar_tensor_tensor(score[:, 1, 0:q], score[:, 0, 0:q], ALPHA, score[:, 0, 0:q],
                                                   ALU.mult, ALU.max).then_inc(back_step, 1)
                else:
                    dve.wait_ge(back_step, 2 * v + 2)
                    if ref >= 1:
                        dve.wait_ge(weights, v)
                    nc.vector.tensor_tensor(score[:, 2, 0:q], score[:, 1, 0:q], rows[:, :, s + 2 + H:s + INFO],
                                            ALU.subtract).then_inc(shifted, 1)

            def weigh(ref, k):
                v, u, q = ref + 2 * k, ref % 2, VISITS[ref].blocks - shared(ref)
                dve.wait_ge(weights, v + 1)
                if ref >= 2:
                    dve.wait_ge(summed, v - 1)
                nc.vector.tensor_tensor(by_head(weighted_h, u, 0, q), by_head(nodes, u, 0, q),
                                        weight[:, u, 0:q].unsqueeze(3).to_broadcast([P, q, H, F]),
                                        ALU.mult).then_inc(weighted, 1)

            def normalise(ref, k, step):
                n = tiles_ended(ref)
                t, u, v = n - 1 + 2 * k, (n - 1) % 2, ref + 2 * k
                if step == 0:
                    dve.wait_ge(summed, v + 1)
                    nc.vector.reciprocal(recip[:], psD[:, u, 0:H]).then_inc(recips, 1)
                    return
                dve.wait_ge(recips, t + 1)
                if n > 2:
                    dve.wait_ge(grown_done, t - 1)
                nc.vector.tensor_tensor(agg[:, u].rearrange("p (h f) -> p h f", h=H), psO[:, u].rearrange("p (h f) -> p h f", h=H),
                                        recip[:].unsqueeze(2).to_broadcast([P, H, F]), ALU.mult).then_inc(agg_done, 1)

            def finish(ref, k, step):
                n = tiles_ended(ref)
                t, u = n - 1 + 2 * k, (n - 1) % 2
                if step == 0:
                    dve.wait_ge(agg_done, t + 1)
                    dve.wait_ge(x_loaded[u], 16 * (((n - 1) // 2) + 1 + k))
                    nc.vector.scalar_tensor_tensor(kept[:, u], agg[:, u], 0.0, x_part[:, u], ALU.max, ALU.add).then_inc(kept_done, 1)
                    return
                dve.wait_ge(grown_done, t + 1)
                dve.wait_ge(kept_done, t + 1)
                if n > 2:
                    dve.wait_ge(stored[u], 16 * (((n - 1) // 2) + k))
                nc.vector.scalar_tensor_tensor(result[:, u], grown[:, u], -1.0, kept[:, u], ALU.add, ALU.add).then_inc(finished, 1)

            def body(ref, k):
                here, ahead, ended = ref < V, ref + 2 < V, ref >= 1 and VISITS[ref - 1].last
                if here:
                    score_edges(ref, k, 0)
                if here:
                    score_edges(ref, k, 1)
                    score_edges(ref, k, 2)
                if ref >= 2 and VISITS[ref - 2].last:
                    finish(ref - 2, k, 1)
                if here:
                    weigh(ref, k)
                if ahead:
                    front(ref + 2, k, 0)
                if ended:
                    normalise(ref - 1, k, 0)
                if ahead:
                    for n in range(1, 5):
                        front(ref + 2, k, n)
                if ended:
                    normalise(ref - 1, k, 1)
                    finish(ref - 1, k, 0)
                if ref + 3 < V:
                    own(ref + 3, k)
            own(0, 0)
            own(1, 0)
            for v in range(2):
                for n in range(5):
                    front(v, 0, n)
            own(2, 0)
            walk(dve, body)
            finish(V - 1, 0, 1)

        @block.tensor
        def _(pe):
            def look_up(ref, k):
                v, u, w = ref + 2 * k, ref % 2, VISITS[ref]
                pe.wait_ge(owners, v + 1)
                if ref >= 2:
                    pe.wait_ge(facts_done, v - 1)
                rows, info = looked(psC, u, w), info_of(ref, k)
                for q in range(w.blocks):
                    mm = nc.tensor.matmul(rows[:, q], owner[:, u, q * P:(q + 1) * P], info, start=True, stop=True)
                mm.then_inc(looked_up, 1)

            def turn_owners(ref, k):
                u, q = ref % 2, VISITS[ref].blocks
                for b in range(0, q, 4):
                    n = min(4, q - b)
                    count = turns(ref - 1) + b // 4
                    step = 0 if isinstance(k, int) else k * (turns(ref + 1) - turns(ref - 1))
                    if count >= 2:
                        pe.wait_ge(to_row_done, count - 1 + step)
                    for j in range(n):
                        mm = nc.tensor.transpose(psR[:, count % 2, j * P:(j + 1) * P], owner[:, u, (b + j) * P:(b + j + 1) * P],
                                                 sb["ident"][:])
                    mm.then_inc(owners_turned, 1)

            def gather_rows(ref, k):
                v, u, w = ref + 2 * k, ref % 2, VISITS[ref]
                n = tiles_ended(ref) if w.last else tiles_ended(ref) + 1
                o = (n - 1) % 2
                pe.wait_ge(weighted, v + 1)
                pe.wait_ge(to_row_done, at(turns, ref, k))
                if n > 2 and w.first:
                    pe.wait_ge(agg_done, n - 2 + 2 * k)
                for q in range(w.blocks):
                    if q == min(4, w.blocks - 1) and ref + 3 < V:
                        look_up(ref + 3, k)
                    a, z = w.first and q == 0, w.last and q == w.blocks - 1
                    if q == w.blocks - 1 and shared(ref):
                        pe.wait_ge(weighted_too, at(shares, ref, k))
                    nc.tensor.matmul(psO[:, o], to_row[:, u, q], weighted_h[:, u, q], start=a, stop=z)
                    mm = nc.tensor.matmul(psD[:, o, 0:H], to_row[:, u, q], weight[:, u, q], start=a, stop=z)
                mm.then_inc(summed, 1)

            def body(ref, k):
                if ref + 1 < V:
                    turn_owners(ref + 1, k)
                if ref < V:
                    gather_rows(ref, k)
            look_up(0, 0)
            look_up(1, 0)
            turn_owners(0, 0)
            look_up(2, 0)
            walk(pe, body)


def lay_out_s2(nc, sb, s2_rows):
    BATCH = 4
    with ExitStack() as ctx:
        s2T = ctx.enter_context(nc.sbuf_tensor([H, N], F32))
        ps = ctx.enter_context(nc.psum_tensor([P, 2, 512], F32))
        transposed = ctx.enter_context(nc.semaphore())
        copied = ctx.enter_context(nc.semaphore())
        copied_odd = ctx.enter_context(nc.semaphore("copied_odd"))
        stored = ctx.enter_context(nc.semaphore())
        stored_too = ctx.enter_context(nc.semaphore("stored_too"))
        block = ctx.enter_context(nc.Block())

        @block.tensor
        def _(pe):
            for b in range(TILES // BATCH):
                if b >= 2:
                    pe.wait_ge(copied_odd if b % 2 else copied, b // 2)
                for j in range(BATCH):
                    mm = nc.tensor.transpose(ps[0:H, b % 2, j * P:(j + 1) * P], S2(sb)[:, b * BATCH + j], sb["ident"][:])
                mm.then_inc(transposed, 1)

        @block.vector
        def _(dve):
            for b in range(0, TILES // BATCH, 2):
                dve.wait_ge(transposed, b + 1)
                nc.vector.tensor_copy(s2T[:, b * 512:(b + 1) * 512], ps[0:H, 0]).then_inc(copied, 1)

        @block.scalar
        def _(act):
            for b in range(1, TILES // BATCH, 2):
                act.wait_ge(transposed, b + 1)
                nc.scalar.activation(s2T[:, b * 512:(b + 1) * 512], ps[0:H, 1], ACT.Copy).then_inc(copied_odd, 1)

        @block.sync
        def _(sp):
            sp.wait_ge(copied, TILES // BATCH // 2)
            sp.wait_ge(copied_odd, TILES // BATCH // 2)
            sp.dma_start(s2_rows[0:H // 2], s2T[0:H // 2]).then_inc(stored, 16)
            sp.wait_ge(stored, 16)

        @block.gpsimd
        def _(pool):
            pool.wait_ge(copied, TILES // BATCH // 2)
            pool.wait_ge(copied_odd, TILES // BATCH // 2)
            pool.dma_start(s2_rows[H // 2:H], s2T[H // 2:H]).then_inc(stored_too, 16)
            pool.wait_ge(stored_too, 16)


def dense_attention(nc, sb, x, adj, table, s2_rows, out):
    PAIR = 2
    PAIRS = H // PAIR
    BANKS = N // 512
    with ExitStack() as ctx:
        s2b = ctx.enter_context(nc.sbuf_tensor([P, PAIR, N], F32))
        h_pair = ctx.enter_context(nc.sbuf_tensor([P, TILES, PAIR * F], F32))
        adj_rows = ctx.enter_context(nc.sbuf_tensor([P, N], I32))
        barred = ctx.enter_context(nc.sbuf_tensor([P, N], F32))
        probs = ctx.enter_context(nc.sbuf_tensor([P, PAIR, N], F32))
        small = ctx.enter_context(nc.sbuf_tensor([P, PAIR, 4], F32))
        rowmax = ctx.enter_context(nc.sbuf_tensor([P, PAIR], F32))
        rowsum = ctx.enter_context(nc.sbuf_tensor([P, PAIR], F32))
        recip = ctx.enter_context(nc.sbuf_tensor([P, PAIR], F32))
        probsT = ctx.enter_context(nc.sbuf_tensor([P, 2, 512], F32))
        x_part = ctx.enter_context(nc.sbuf_tensor([P, PAIR * F], F32))
        fin = ctx.enter_context(nc.sbuf_tensor([P, 4, PAIR * F], F32))
        psT = ctx.enter_context(nc.psum_tensor([P, 2, 512], F32))
        psO = ctx.enter_context(nc.psum_tensor([P, 2, 512], F32))
        sem = lambda name: ctx.enter_context(nc.semaphore(name))
        pair_loaded, adj_loaded, x_loaded = sem("pair_loaded"), sem("adj_loaded"), sem("x_loaded")
        barred_done, scores_done = sem("barred_done"), sem("scores_done")
        max_part, max_done = sem("max_part"), sem("max_done")
        leaky_done, probs_done = sem("leaky_done"), sem("probs_done")
        transposed, probsT_done, summed_bank = sem("transposed"), sem("probsT_done"), sem("summed_bank")
        fin_part, fin_neg, fin_exp, fin_done = sem("fin_part"), sem("fin_neg"), sem("fin_exp"), sem("fin_done")
        stored = sem("stored")
        block = ctx.enter_context(nc.Block())
        adjt = adj.rearrange("(t p) n -> t p n", p=P)

        @block.sync
        def _(sp):
            sp.sem_inc(stored, 16)
            with sp.Fori(0, PAIRS) as g:
                sp.wait_ge(fin_done, g * TILES + 1)
                for u in range(PAIR):
                    sp.dma_start(s2b[:, u], broadcast_rows(s2_rows[bass.ds(g * PAIR + u, 1)][0])).then_inc(pair_loaded, 16)
                sp.dma_start(h_pair[:], table[0:N].rearrange("(t p) d -> p t d", p=P)[:, :, bass.ds(g * PAIR * F, PAIR * F)]
                             ).then_inc(pair_loaded, 16)
                with sp.Fori(0, TILES) as t:
                    step = g * TILES + t
                    sp.wait_ge(barred_done, step + 1)
                    sp.dma_start(adj_rows[:], adjt[bass.ds(t, 1)][0]).then_inc(adj_loaded, 16)
                    sp.wait_ge(fin_done, step + 1)
                    sp.dma_start(x_part[:], x.rearrange("(t p) d -> t p d", p=P)[bass.ds(t, 1)][0][:, bass.ds(g * PAIR * F, PAIR * F)]
                                 ).then_inc(x_loaded, 16)
                    sp.wait_ge(fin_done, step + 2)
                    sp.dma_start(out.rearrange("(t p) d -> t p d", p=P)[bass.ds(t, 1)][0][:, bass.ds(g * PAIR * F, PAIR * F)],
                                 fin[:, 3]).then_inc(stored, 16)
            sp.wait_ge(stored, 16 * PAIRS * TILES + 16)

        @block.vector
        def _(dve):
            for ahead in (fin_done, barred_done, scores_done, fin_neg):
                dve.sem_inc(ahead, 1)
            with dve.Fori(0, PAIRS) as g:
                with dve.Fori(0, TILES) as t:
                    step = g * TILES + t
                    dve.wait_ge(pair_loaded, 48 * g + 48)
                    dve.wait_ge(adj_loaded, 16 * step + 16)
                    dve.wait_ge(scores_done, 2 * step + 1)
                    nc.vector.tensor_scalar(barred[:], adj_rows[:], 0.0, NEG_BIG, ALU.is_le, ALU.mult).then_inc(barred_done, 1)
                    dve.wait_ge(barred_done, step + 2)
                    dve.wait_ge(summed_bank, 2 * BANKS * step + 1)
                    for u in range(PAIR):
                        s1 = S1(sb)[:, bass.ds(t, 1), bass.ds(g * PAIR + u, 1)].rearrange("p a b -> p (a b)")
                        nc.vector.scalar_tensor_tensor(probs[:, u], barred[:], s1, s2b[:, u], ALU.add, ALU.add).then_inc(scores_done, 1)
                        dve.wait_ge(scores_done, 2 * step + u + 2)
                        nc.vector.scalar_tensor_tensor(probs[:, u], probs[:, u], ALPHA, probs[:, u],
                                                       ALU.mult, ALU.max).then_inc(leaky_done, 1)
                        dve.wait_ge(leaky_done, 2 * step + u + 1)
                        nc.vector.tensor_reduce(small[:, u, 0:1], probs[:, u], AX.X, ALU.max).then_inc(max_part, 1)
                        dve.wait_ge(max_part, 2 * step + u + 1)
                        nc.vector.tensor_scalar(rowmax[:, u:u + 1], small[:, u, 0:1], -1.0, None, ALU.mult).then_inc(max_done, 1)
                    for u in range(PAIR):
                        for b in range(BANKS):
                            k = 2 * BANKS * step + u * BANKS + b
                            dve.wait_ge(transposed, k + 1)
                            if u * BANKS + b >= 2:
                                dve.wait_ge(summed_bank, k)
                            nc.vector.tensor_copy(probsT[:, b % 2], psT[:, b % 2]).then_inc(probsT_done, 1)
                    dve.wait_ge(probs_done, 2 * step + 2)
                    nc.vector.reciprocal(recip[:], rowsum[:]).then_inc(fin_part, 1)
                    dve.wait_ge(summed_bank, 2 * BANKS * step + 2 * BANKS + 1)
                    dve.wait_ge(fin_part, 3 * step + 1)
                    dve.wait_ge(stored, 16 * step + 16)
                    for u in range(PAIR):
                        nc.vector.tensor_scalar(fin[:, 0, u * F:(u + 1) * F], psO[:, u, 0:F], recip[:, u:u + 1], None,
                                                ALU.mult).then_inc(fin_part, 1)
                    dve.wait_ge(fin_part, 3 * step + 3)
                    nc.vector.tensor_scalar(fin[:, 1], fin[:, 0], 0.0, None, ALU.min).then_inc(fin_neg, 1)
                    dve.wait_ge(x_loaded, 16 * step + 16)
                    nc.vector.scalar_tensor_tensor(fin[:, 3], fin[:, 0], 0.0, x_part[:], ALU.max, ALU.add).then_inc(fin_neg, 1)
                    dve.wait_ge(fin_neg, 2 * step + 3)
                    dve.wait_ge(fin_exp, step + 1)
                    nc.vector.scalar_tensor_tensor(fin[:, 3], fin[:, 2], -1.0, fin[:, 3], ALU.add, ALU.add).then_inc(fin_done, 1)

        @block.scalar
        def _(act):
            with act.Fori(0, PAIRS) as g:
                with act.Fori(0, TILES) as t:
                    step = g * TILES + t
                    for u in range(PAIR):
                        act.wait_ge(max_done, 2 * step + u + 1)
                        nc.scalar.activation(probs[:, u], probs[:, u], ACT.Exp, bias=rowmax[:, u:u + 1],
                                             accum_out=rowsum[:, u:u + 1]).then_inc(probs_done, 1)
                    act.wait_ge(fin_neg, 2 * step + 2)
                    nc.scalar.activation(fin[:, 2], fin[:, 1], ACT.Exp).then_inc(fin_exp, 1)

        @block.tensor
        def _(pe):
            pe.sem_inc(summed_bank, 1)
            with pe.Fori(0, PAIRS) as g:
                with pe.Fori(0, TILES) as t:
                    step = g * TILES + t
                    pe.wait_ge(pair_loaded, 48 * g + 48)
                    pe.wait_ge(fin_neg, 2 * step + 1)
                    for u in range(PAIR):
                        pe.wait_ge(probs_done, 2 * step + u + 1)

                        def turn_bank(b):
                            k = 2 * BANKS * step + u * BANKS + b
                            if u * BANKS + b >= 2:
                                pe.wait_ge(probsT_done, k - 1)
                            for j in range(4):
                                mm = nc.tensor.transpose(psT[:, b % 2, j * P:(j + 1) * P],
                                                         probs[:, u, (4 * b + j) * P:(4 * b + j + 1) * P], sb["ident"][:])
                            mm.then_inc(transposed, 1)

                        def sum_bank(b):
                            k = 2 * BANKS * step + u * BANKS + b
                            pe.wait_ge(probsT_done, k + 1)
                            for j in range(4):
                                mm = nc.tensor.matmul(psO[:, u, 0:F], probsT[:, b % 2, j * P:(j + 1) * P],
                                                      h_pair[:, 4 * b + j, u * F:(u + 1) * F],
                                                      start=(b == 0 and j == 0), stop=(b == BANKS - 1 and j == 3))
                            mm.then_inc(summed_bank, 1)
                            return mm
                        turn_bank(0)
                        for b in range(BANKS):
                            if b + 1 < BANKS:
                                turn_bank(b + 1)
                            mm = sum_bank(b)


def build(nc, x, adj, W, a1, a2, out):
    table = nc.dram_tensor("table", (N + 1, TABLE), F32).ap()
    s2_rows = nc.dram_tensor("s2_rows", (H, N), F32).ap()
    with ExitStack() as ctx:
        def buf(name, shape, dtype=F32):
            return ctx.enter_context(nc.sbuf_tensor(name, shape, dtype))
        sb = {name: buf(name, shape) for name, shape in (("ident", [P, P]), ("ones", [P, P]),
                                                         ("s12", [P, 2, TILES, H]))}
        sb["flag"] = buf("flag", [1, 1], I32)
        with ExitStack() as edges:
            def tmp(name, shape, dtype=F32):
                sb[name] = edges.enter_context(nc.sbuf_tensor(name, shape, dtype))
            for kind in "ABC":
                tmp("info" + kind, [P, COUNT[kind], SLOTS[kind] + INFO])
            tmp("fullest", [P, V])
            tmp("neg_centre", [P, V])
            tmp("half_sq", [P, V])
            tmp("node_sum", [P, HF])
            with ExitStack() as scan:
                for name, shape, dtype in (("W", [P, KC, HF], F32), ("Wa", [P, KC, 2 * H], F32),
                                           ("step_diag", [P, P], BF16), ("radix", [33, P], BF16),
                                           ("digits", [33, N], BF16),
                                           ("x_rows", [P, 2, D], F32), ("adj_rows", [P, 2, N], I32)):
                    sb[name] = scan.enter_context(nc.sbuf_tensor("sb_" + name, shape, dtype))
                for name in ("x_loaded", "adj_loaded"):
                    sb[name] = [scan.enter_context(nc.semaphore(f"{name}{u}")) for u in range(2)]
                setup(nc, sb, x, adj, W, a1, a2)
                project_and_scan(nc, sb, x, adj, table)
            plan(nc, sb, table)
            attend_edges(nc, sb, x, table, out)
        flag = nc.values_load(sb["flag"][0:1, 0:1], min_val=0, max_val=1, skip_runtime_bounds_check_because="a comparison wrote it")
        with nc.If(flag > 0):
            lay_out_s2(nc, sb, s2_rows)
            dense_attention(nc, sb, x, adj, table, s2_rows, out)


_INS = ['x', 'adj', 'L0_gnn_W', 'L0_gnn_a1', 'L0_gnn_a2']
_OUTS = [((6144, 512), 'float32')]


def kernel(**inputs):
    import numpy as _np
    import concourse.bacc as _bacc
    from concourse import mybir as _mybir
    from concourse.bass_utils import run_bass_kernel_spmd as _run

    nc = _bacc.Bacc("TRN2", target_bir_lowering=False, num_devices=1)
    arrays, args = {}, []
    for name in _INS:
        a = _np.ascontiguousarray(inputs[name])
        arrays[f"in_{name}_dram"] = a
        args.append(nc.dram_tensor(f"in_{name}_dram", a.shape, _mybir.dt.from_np(a.dtype), kind="ExternalInput").ap())
    for i, (shape, dtype) in enumerate(_OUTS):
        dt = _mybir.dt.from_np(_np.dtype(dtype))
        args.append(nc.dram_tensor(f"out_{i}_dram", shape, dt, kind="ExternalOutput").ap())
    build(nc, *args)
    r = _run(nc, [arrays], core_ids=[0])
    got = tuple(r.results[0][f"out_{i}_dram"] for i in range(len(_OUTS)))
    return got[0]
```
